# Optimizing a Trainium2 kernel written in Bass

```python
import numpy as np
import jax
import jax.numpy as jnp

def _softmax(x, axis=-1):
    return jax.nn.softmax(x, axis=axis)

def _gelu(x):
    return jax.nn.gelu(x, approximate=True)

def _silu(x):
    return jax.nn.silu(x)

def _sigmoid(x):
    return jax.nn.sigmoid(x)

def _layernorm(x, axis=-1, eps=1e-05):
    m = jnp.mean(x, axis=axis, keepdims=True)
    v = jnp.var(x, axis=axis, keepdims=True)
    return (x - m) / jnp.sqrt(v + eps)

def _scatter_add(tgt, idx, src, axis=0):
    return tgt.at[idx].add(src)

def _segment_sum(src, seg, n):
    return jax.ops.segment_sum(src, seg, n)
kernel_name = 'mk_gnn_resnorm_d2_gnn_r8_790b30'

def setup_inputs(seed: int=0):
    np.random.seed(seed)
    _w = jnp.asarray

    def _rec_inputs():
        import jax
        import jax.numpy as jnp
        _gk = jax.random.key(seed)
        x = -0.0002117 + 1 * jax.random.normal(jax.random.fold_in(_gk, 1), (1250, 1024), jnp.float32)
        src = jax.random.randint(jax.random.fold_in(_gk, 2), (20000,), 0, 1250, jnp.int32)
        dst = jax.random.randint(jax.random.fold_in(_gk, 3), (20000,), 0, 1250, jnp.int32)
        _o = jnp.argsort(dst, stable=True)
        src = src[_o]
        dst = dst[_o]
        return (x, src, dst)
    x, src, dst = _rec_inputs()

    def _L0_gnn_setup():
        import jax, jax.numpy as jnp
        import numpy as np
        N_NODES = 3125
        N_EDGES = 50000
        D = 1024

        def _sage_layer(h, edge_src, edge_dst, deg_inv, W_self, W_neigh, b):
            msg = h[edge_src]
            agg = jax.ops.segment_sum(msg, edge_dst, num_segments=h.shape[0])
            mean = agg * deg_inv[:, None]
            return h @ W_self + mean @ W_neigh + b
        key = jax.random.key(seed)
        ks = jax.random.split(key, 8)
        s = 1.0 / np.sqrt(D)
        return {'x': jax.random.normal(ks[0], (N_NODES, D), dtype=jnp.float32), 'edge_src': jax.random.randint(ks[1], (N_EDGES,), 0, N_NODES, dtype=jnp.int32), 'edge_dst': jax.random.randint(ks[2], (N_EDGES,), 0, N_NODES, dtype=jnp.int32), 'W_self0': jax.random.normal(ks[3], (D, D), dtype=jnp.float32) * s, 'W_neigh0': jax.random.normal(ks[4], (D, D), dtype=jnp.float32) * s, 'b0': jnp.zeros((D,), dtype=jnp.float32), 'W_self1': jax.random.normal(ks[5], (D, D), dtype=jnp.float32) * s, 'W_neigh1': jax.random.normal(ks[6], (D, D), dtype=jnp.float32) * s, 'b1': jnp.zeros((D,), dtype=jnp.float32)}
    _L0_gnn_all = _L0_gnn_setup()
    _L0_gnn_in = {k: v for k, v in _L0_gnn_all.items() if k in ('W_self0', 'W_neigh0', 'b0', 'W_self1', 'W_neigh1', 'b1')}
    del _L0_gnn_all

    def _L1_gnn_setup():
        import jax, jax.numpy as jnp
        import numpy as np
        N = 2500
        E = 40000
        D_IN = 1024
        D_OUT = 1024
        key = jax.random.key(seed)
        k1, k2, k3, k4 = jax.random.split(key, 4)
        x = jax.random.normal(k1, (N, D_IN), dtype=jnp.float32)
        edge_index = jax.random.randint(k2, (2, E), 0, N, dtype=jnp.int64)
        W = jax.random.normal(k3, (D_OUT, D_IN), dtype=jnp.float32) * (1.0 / np.sqrt(D_IN))
        b = jax.random.normal(k4, (D_OUT,), dtype=jnp.float32) * 0.01
        return {'x': x, 'edge_index': edge_index, 'W': W, 'b': b}
    _L1_gnn_all = _L1_gnn_setup()
    _L1_gnn_in = {k: v for k, v in _L1_gnn_all.items() if k in ('W', 'b')}
    del _L1_gnn_all
    return {'x': x, 'src': src, 'dst': dst, 'L0_gnn_W_self0': _L0_gnn_in['W_self0'], 'L0_gnn_W_neigh0': _L0_gnn_in['W_neigh0'], 'L0_gnn_b0': _L0_gnn_in['b0'], 'L0_gnn_W_self1': _L0_gnn_in['W_self1'], 'L0_gnn_W_neigh1': _L0_gnn_in['W_neigh1'], 'L0_gnn_b1': _L0_gnn_in['b1'], 'L1_gnn_W': _L1_gnn_in['W'], 'L1_gnn_b': _L1_gnn_in['b']}

def reference(x, src, dst, L0_gnn_W_self0, L0_gnn_W_neigh0, L0_gnn_b0, L0_gnn_W_self1, L0_gnn_W_neigh1, L0_gnn_b1, L1_gnn_W, L1_gnn_b):
    import jax
    import jax.numpy as jnp

    def _L0_gnn_ref(x, edge_src, edge_dst, W_self0, W_neigh0, b0, W_self1, W_neigh1, b1):
        import jax, jax.numpy as jnp
        import numpy as np
        N_NODES = 3125
        N_EDGES = 50000
        D = 1024

        def _sage_layer(h, edge_src, edge_dst, deg_inv, W_self, W_neigh, b):
            msg = h[edge_src]
            agg = jax.ops.segment_sum(msg, edge_dst, num_segments=h.shape[0])
            mean = agg * deg_inv[:, None]
            return h @ W_self + mean @ W_neigh + b
        N = x.shape[0]
        deg = jax.ops.segment_sum(jnp.ones_like(edge_dst, dtype=x.dtype), edge_dst, num_segments=N)
        deg_inv = 1.0 / jnp.maximum(deg, 1.0)
        h = jax.nn.relu(_sage_layer(x, edge_src, edge_dst, deg_inv, W_self0, W_neigh0, b0))
        out = _sage_layer(h, edge_src, edge_dst, deg_inv, W_self1, W_neigh1, b1)
        return out

    def _L1_gnn_ref(x, edge_index, W, b):
        import jax, jax.numpy as jnp
        import numpy as np
        N = 2500
        E = 40000
        D_IN = 1024
        D_OUT = 1024
        num_nodes = x.shape[0]
        self_idx = jnp.arange(num_nodes, dtype=edge_index.dtype)
        ei = jnp.concatenate([edge_index, jnp.stack([self_idx, self_idx], axis=0)], axis=1)
        row, col = (ei[0], ei[1])
        h = jnp.einsum('nd,od->no', x, W) + b
        deg = jnp.zeros((num_nodes,), dtype=h.dtype).at[row].add(1.0)
        deg_inv_sqrt = deg ** (-0.5)
        norm = deg_inv_sqrt[row] * deg_inv_sqrt[col]
        msg = norm[:, None] * h[col]
        out = jax.ops.segment_sum(msg, row, num_segments=num_nodes)
        return out
    edge_index = jnp.stack([src, dst])
    x = _layernorm(x + _L0_gnn_ref(x, src, dst, L0_gnn_W_self0, L0_gnn_W_neigh0, L0_gnn_b0, L0_gnn_W_self1, L0_gnn_W_neigh1, L0_gnn_b1), axis=-1)
    x = _layernorm(x + _L1_gnn_ref(x, edge_index, L1_gnn_W, L1_gnn_b), axis=-1)
    return x

_drawn_inputs = setup_inputs


def setup_inputs(seed=0):
    import zlib

    import numpy as np

    out = dict(_drawn_inputs(seed))
    spreads = {'L0_gnn_b0': (0.0, 0.1), 'L0_gnn_b1': (0.0, 0.1)}
    factors = {'L1_gnn_b': 6.73}
    for name, (base, spread) in spreads.items():
        noise = np.random.default_rng([zlib.crc32(name.encode()), seed]).standard_normal(out[name].shape)
        drawn = base * np.exp(spread * noise) if base else spread * noise
        out[name] = jnp.asarray(drawn.astype(out[name].dtype))
    for name, factor in factors.items():
        out[name] = (out[name] * factor).astype(out[name].dtype)
    return out
```

```python
from contextlib import ExitStack

import concourse.bass as bass
from concourse import mybir

P = 128
PSUM_COLS = 512
WINDOW = 48
NO_NODE = 4095
SKIP = 1 << 22
KEY_SHIFT = 2048
EPS = 1e-5

F32 = mybir.dt.float32
F32R = mybir.dt.float32r
I32 = mybir.dt.int32
ACT = mybir.ActivationFunctionType
ALU = mybir.AluOpType
AX_X = mybir.AxisListType.X


def build(nc, x, src, dst, w_self0, w_neigh0, b0, w_self1, w_neigh1, b1, w_gcn, b_gcn, out):
    N, D = x.shape
    E = src.shape[0]
    NT = -(-N // P)
    LAST = N - (NT - 1) * P
    KD = D // P
    NC = D // PSUM_COLS
    EP = 125
    EC = E // EP
    BATCH = EC // NT
    SLOTS = 2
    PAIRS = NT // SLOTS
    BLOCK = NT * P
    CELLS = NT * P * BLOCK
    HALO = EC + 2 * WINDOW
    PAIR_KEYS = BLOCK // EC
    ZEROS = 2 * P
    KEY_LOAD = 1000
    assert E == EP * EC and EC % NT == 0 and NT % SLOTS == 0 and KD % SLOTS == 0
    assert E % KEY_LOAD == 0 and KEY_LOAD % PAIR_KEYS == 0 and KEY_LOAD <= D
    assert BATCH * WINDOW <= BLOCK and N < KEY_SHIFT - 1 and SKIP > CELLS

    NEIGH0, SELF0, MEAN0, NEIGH1, SELF1, MEAN1, GCN_LIN, GCN_AGG = range(8)
    LIN = {NEIGH0: 0, SELF0: 1, NEIGH1: 2, SELF1: 3, GCN_LIN: 4}
    AGG = {MEAN0: 0, MEAN1: 1, GCN_AGG: 2}
    STORE = {SELF0: 0, MEAN0: 1, SELF1: 2, MEAN1: 3, GCN_AGG: 4}

    with ExitStack() as ctx:
        def sb(name, shape, dt):
            return ctx.enter_context(nc.sbuf_tensor(name, shape, dt))

        def sem(name):
            return ctx.enter_context(nc.semaphore(name))

        def dram(name, shape, dt=F32):
            return nc.dram_tensor(name, shape, dt, kind="Internal").ap()

        self_scr = dram("self_scr", [NT * P, D])
        h_scr = dram("h_scr", [NT * P, D])
        y_scr = dram("y_scr", [NT * P, D])
        keys_scr = dram("keys_scr", [E])
        adj_in = dram("adj_in", [CELLS, 1])
        adj_out = dram("adj_out", [CELLS, 1])

        u_hi = sb("u_hi", [P, NT, D], F32R)
        u_lo = sb("u_lo", [P, NT, D], F32R)
        w_hi = sb("w_hi", [P, KD, D], F32R)
        w_lo = sb("w_lo", [P, KD, D], F32R)
        xt_hi = sb("xt_hi", [P, SLOTS, D], F32R)
        xt_lo = sb("xt_lo", [P, SLOTS, D], F32R)
        adj = sb("adj", [P, SLOTS, BLOCK], F32R)
        ones = sb("ones", [P, 2], F32R)

        xin = sb("xin", [P, SLOTS, D], F32)
        raw = sb("raw", [P, SLOTS, D], F32)
        outb = sb("outb", [P, SLOTS, D], F32)
        bias = sb("bias", [P, D], F32)
        zeros = sb("zeros", [P, ZEROS], F32)
        ident = sb("ident", [P, P], F32)
        key = sb("key", [P, HALO], F32)
        idx_in = sb("idx_in", [P, EC], I32)
        idx_out = sb("idx_out", [P, EC], I32)
        mult = sb("mult", [P, EC], F32)
        pairs = sb("pairs", [P, EC], F32)
        repeat = sb("repeat", [P, 4, BATCH], F32)
        idx_slot = sb("idx_slot", [P, SLOTS, BATCH], I32)
        mult_slot = sb("mult_slot", [P, SLOTS, BATCH], F32)
        bad = sb("bad", [P, 4], F32)
        flag = sb("flag", [P, 2], I32)
        dinv = sb("dinv", [P, NT], F32)
        degc = sb("degc", [P, SLOTS], F32)
        dsum = sb("dsum", [P, NT], F32)
        dpart = sb("dpart", [P, SLOTS, NT], F32)
        dsqrt = sb("dsqrt", [P, NT], F32)
        dscale = sb("dscale", [P, NT], F32)
        stats = sb("stats", [P, SLOTS, NC, 6], F32)
        mv = sb("mv", [P, SLOTS, 2], F32)
        std = sb("std", [P, SLOTS], F32)
        rstd = sb("rstd", [P, SLOTS], F32)
        eps = sb("eps", [P, 1], F32)
        scrap_dve = sb("scrap_dve", [P, 1], F32)
        scrap_pool = sb("scrap_pool", [P, 1], F32)
        ones_f = sb("ones_f", [P, 1], F32)

        e_dst = outb[:, 0, 0:HALO].bitcast(I32)
        e_src = outb[:, 0, HALO:2 * HALO].bitcast(I32)
        part = [outb[:, 1, i * EC:(i + 1) * EC].bitcast(I32) for i in range(4)]
        sums = [outb[:, 0, 2 * HALO + i * EC:2 * HALO + (i + 1) * EC] for i in range(2)]
        assert 2 * HALO + 2 * EC <= D and 4 * EC <= D

        acc = ctx.enter_context(nc.psum_tensor("acc", [P, SLOTS, D], F32))
        turned = ctx.enter_context(nc.psum_tensor("turned", [P, D], F32))
        count = ctx.enter_context(nc.psum_tensor("count", [P, SLOTS, PSUM_COLS], F32))

        edges_in = sem("edges_in")
        halo_set = sem("halo_set")
        ident_zero = sem("ident_zero")
        ident_ready = sem("ident_ready")
        ones_ready = sem("ones_ready")
        zeros_ready = sem("zeros_ready")
        cleared_in = sem("cleared_in")
        cleared_out = sem("cleared_out")
        prep = sem("prep")
        bad_ready = sem("bad_ready")
        bad_summed = sem("bad_summed")
        flag_ready = sem("flag_ready")
        keys_out = sem("keys_out")
        keys_in = sem("keys_in")
        keys_used = sem("keys_used")
        pair_eq = sem("pair_eq")
        pair_sum = sem("pair_sum")
        same = sem("same")
        batch_ready = sem("batch_ready")
        batch_copied = sem("batch_copied")
        scattered = [sem(f"scattered{s}") for s in range(SLOTS)]
        wt_turned = sem("wt_turned")
        xin_full = [sem(f"xin_full{s}") for s in range(SLOTS)]
        raw_full = [sem(f"raw_full{s}") for s in range(SLOTS)]
        adj_full = [sem(f"adj_full{s}") for s in range(SLOTS)]
        stored = [sem(f"stored{s}") for s in range(SLOTS)]
        bias_full = sem("bias_full")
        xt_turned = sem("xt_turned")
        xt_hi_done = sem("xt_hi_done")
        xt_lo_done = sem("xt_lo_done")
        w_hi_done = sem("w_hi_done")
        w_lo_done = sem("w_lo_done")
        w_used = sem("w_used")
        acc_full = sem("acc_full")
        acc_free = sem("acc_free")
        u_hi_done = sem("u_hi_done")
        u_lo_done = sem("u_lo_done")
        res_done = sem("res_done")
        deg_step = sem("deg_step")
        dsum_zero = sem("dsum_zero")
        dsum_part = sem("dsum_part")
        dsum_done = sem("dsum_done")
        dsqrt_done = sem("dsqrt_done")
        dscale_done = sem("dscale_done")
        relu_done = sem("relu_done")
        loop_added = sem("loop_added")
        z_done = sem("z_done")
        stats_done = sem("stats_done")
        mv_done = sem("mv_done")
        std_done = sem("std_done")
        rstd_done = sem("rstd_done")
        norm_done = sem("norm_done")
        eps_ready = sem("eps_ready")

        sources = {NEIGH0: x, SELF0: x, MEAN0: self_scr, NEIGH1: h_scr, SELF1: h_scr, MEAN1: self_scr,
                   GCN_LIN: y_scr, GCN_AGG: y_scr}
        made_by = {MEAN0: SELF0, NEIGH1: MEAN0, SELF1: MEAN0, MEAN1: SELF1, GCN_LIN: MEAN1, GCN_AGG: MEAN1}
        results = {SELF0: self_scr, MEAN0: h_scr, SELF1: self_scr, MEAN1: y_scr, GCN_AGG: out}
        weights = [w_neigh0, w_self0, w_neigh1, w_self1, w_gcn]
        biases = {SELF0: b0, SELF1: b1, GCN_LIN: b_gcn}

        def rows(t):
            return LAST if isinstance(t, int) and t == NT - 1 else P

        def tiles(eng, body):
            with eng.Fori(0, PAIRS - 1) as i:
                for s in range(SLOTS):
                    body(i * SLOTS + s, i, s, i * SLOTS + s)
            for s in range(SLOTS):
                body(NT - SLOTS + s, PAIRS - 1, s, None)

        def row(buf, t):
            return buf[:, bass.ds(t, 1), :].rearrange("p a d -> p (a d)")

        def turned_part(buf, c):
            return buf[:, :, bass.ds(c * P, P)]

        block = ctx.enter_context(nc.Block())

        @block.sync
        def _(sp):
            def load_weights(l, c, s):
                if l == LIN[GCN_LIN] and isinstance(c, int) and c < SLOTS:
                    sp.wait_ge(res_done, NT - SLOTS + s + 1)
                elif l > 0 or c >= SLOTS:
                    sp.wait_ge(w_lo_done, l * KD + c - SLOTS + 1)
                sp.dma_start(raw[:, s, :], weights[l][bass.ds(c * P, P), :]).then_inc(raw_full[s], 16)

            def load_tile(q, t, pair, s):
                before, t_before = (q, t - SLOTS) if not isinstance(t, int) or t >= SLOTS else (q - 1, NT - SLOTS + s)
                if before == GCN_AGG:
                    sp.wait_ge(z_done, t_before + 1)
                elif before in LIN:
                    sp.wait_ge(xt_turned, LIN[before] * NT + t_before + 1)
                elif before in AGG:
                    sp.wait_ge(acc_free, SLOTS + before * NT + t_before + 1)
                if q in made_by:
                    sp.wait_ge(stored[s], 16 * (STORE[made_by[q]] * PAIRS + pair + 2))
                n = rows(t) if sources[q] is x else P
                sp.dma_start(xin[0:n, s, :], sources[q][bass.ds(t * P, n), :]).then_inc(xin_full[s], 16)

            def load_adj(q, t, s):
                if isinstance(t, int) and t < SLOTS and q != MEAN0:
                    sp.wait_ge(acc_full, ({MEAN1: MEAN0, GCN_AGG: MEAN1}[q] + 1) * NT)
                    sp.wait_ge(dsum_part, NT)
                table = (adj_out if q == GCN_AGG else adj_in).rearrange("(a p b) o -> a p (b o)", p=P, b=BLOCK)
                sp.dma_start(adj[:, s, :].bitcast(F32), table[bass.ds(t, 1), :, :].rearrange("a p b -> (a p) b")
                             ).then_inc(adj_full[s], 16)

            def load_residual(t, s):
                if isinstance(t, int) and t < SLOTS:
                    sp.wait_ge(w_lo_done, (LIN[SELF1] + 1) * KD)
                else:
                    sp.wait_ge(res_done, t - SLOTS + 1)
                n = rows(t)
                sp.dma_start(raw[0:n, s, :], x[bass.ds(t * P, n), :]).then_inc(raw_full[s], 16)

            def load_bias(q):
                if q == SELF0:
                    sp.wait_ge(flag_ready, 2)
                else:
                    sp.wait_ge(acc_free, SLOTS + ({SELF1: SELF0, GCN_LIN: SELF1}[q] + 1) * NT)
                sp.dma_start(bias[:, :], biases[q].rearrange("(a d) -> a d", a=1).broadcast_to([P, D])).then_inc(bias_full, 16)

            def first_tiles(q):
                for s in range(SLOTS):
                    load_tile(q, s, 0, s)
                    if q in AGG:
                        load_adj(q, s, s)
                        if q + 1 in LIN:
                            load_weights(LIN[q + 1], s, s)
                    if q == SELF1:
                        load_residual(s, s)

            def other_tiles(q):
                def body(t, pair, s):
                    load_tile(q, t, pair, s)
                    if q in AGG:
                        load_adj(q, t, s)
                        if q + 1 in LIN and not isinstance(t, int):
                            load_weights(LIN[q + 1], t, s)
                    if q == SELF1:
                        load_residual(t, s)
                with sp.Fori(1, PAIRS - 1) as i:
                    for s in range(SLOTS):
                        body(i * SLOTS + s, i, s)
                for s in range(SLOTS):
                    body(NT - SLOTS + s, PAIRS - 1, s)

            sp.wait_ge(halo_set, 2)
            for ids, where in ((dst, e_dst), (src, e_src)):
                grid = ids.rearrange("(p c) -> p c", c=EC)
                sp.dma_start(where[0:EP, WINDOW:WINDOW + EC], grid).then_inc(edges_in, 16)
                sp.dma_start(where[1:EP, 0:WINDOW], grid[0:EP - 1, EC - WINDOW:EC]).then_inc(edges_in, 16)
                sp.dma_start(where[0:EP - 1, WINDOW + EC:HALO], grid[1:EP, 0:WINDOW]).then_inc(edges_in, 16)
            load_tile(NEIGH0, 0, 0, 0)
            for c in range(KD):
                load_weights(0, c, c % SLOTS)
                if c == 1:
                    load_tile(NEIGH0, 1, 0, 1)
            other_tiles(NEIGH0)
            for q in range(1, 8):
                if q in LIN and q - 1 in LIN:
                    for c in range(SLOTS):
                        load_weights(LIN[q], c, c)
                    for s in range(SLOTS):
                        load_tile(q, s, 0, s)
                    for c in range(SLOTS, KD):
                        load_weights(LIN[q], c, c % SLOTS)
                    if q == SELF1:
                        for s in range(SLOTS):
                            load_residual(s, s)
                else:
                    if q == MEAN0:
                        for s in range(SLOTS):
                            sp.wait_ge(scattered[s], 16 * EC // SLOTS)
                    if q == GCN_AGG:
                        for s in range(SLOTS):
                            sp.wait_ge(scattered[s], 16 * EC)
                    first_tiles(q)
                if q in biases:
                    load_bias(q)
                other_tiles(q)
            for s in range(SLOTS):
                sp.wait_ge(stored[s], 16 * ((STORE[GCN_AGG] + 1) * PAIRS + 1))

        @block.gpsimd
        def _(pool):
            nc.gpsimd.memset(e_dst[0:EP, :], NO_NODE).then_inc(halo_set, 1)
            nc.gpsimd.memset(e_src[0:EP, :], NO_NODE).then_inc(halo_set, 1)
            nc.gpsimd.memset(ident[:, :], 0.0).then_inc(ident_zero, 1)
            pool.wait_ge(ident_zero, 1)
            nc.gpsimd.affine_select(out=ident[:, :], in_=ident[:, :], compare_op=ALU.not_equal, fill=1.0, base=0,
                                    pattern=[[-1, P]], channel_multiplier=1).then_inc(ident_ready, 1)
            nc.gpsimd.memset(zeros[:, :], 0.0).then_inc(zeros_ready, 1)
            pool.wait_ge(zeros_ready, 1)

            def clear(table, done):
                blocks = table.rearrange("(a p b) o -> a p (b o)", p=P, b=BLOCK)
                for a in range(NT):
                    pool.dma_start(blocks[a].rearrange("p (c z) -> p c z", z=ZEROS), zeros[:, :].unsqueeze(1).broadcast_to([P, BLOCK // ZEROS, ZEROS])).then_inc(done, 16)

            def scatter(table, cleared, index, scattered_before):
                def batch(i, s):
                    b = i * SLOTS + s
                    pool.wait_ge(batch_ready, b + 1)
                    if scattered_before or not isinstance(i, int):
                        pool.wait_ge(scattered[s], (i + scattered_before * PAIRS) * (16 * BATCH))
                    cols = bass.ds(b * BATCH, BATCH)
                    nc.gpsimd.tensor_copy(idx_slot[0:EP, s, :], index[0:EP, cols]).then_inc(batch_copied, 1)
                    nc.gpsimd.tensor_copy(mult_slot[0:EP, s, :], mult[0:EP, cols]).then_inc(batch_copied, 1)
                    pool.wait_ge(cleared, 16 * NT)
                    pool.wait_ge(batch_copied, (b + 1 + scattered_before * NT) * 2)
                    nc.gpsimd.tensor_tensor(scrap_pool[0:EP, :], mult_slot[0:EP, s, 0:1], mult_slot[0:EP, s, 0:1], ALU.add)
                    for j in range(BATCH):
                        pool.indirect_dma_start(
                            table, bass.IndirectOffsetOnAxis(ap=idx_slot[0:EP, s, j:j + 1], axis=0),
                            mult_slot[0:EP, s, j:j + 1], None, bounds_check=CELLS - 1, oob_is_err=False,
                        ).then_inc(scattered[s], 16)

                for s in range(SLOTS):
                    batch(0, s)
                with pool.Fori(1, PAIRS) as i:
                    for s in range(SLOTS):
                        batch(i, s)

            pool.wait_ge(flag_ready, 1)
            general = pool.value_load(flag[0:1, 0:1], min_val=0, max_val=1)
            with pool.If(general > 0):
                pool.dma_start(keys_scr.rearrange("(p c) -> p c", c=EC), key[0:EP, WINDOW:WINDOW + EC]).then_inc(keys_out, 16)
                pool.wait_ge(keys_out, 16)
                spread = keys_scr.rearrange("(n k) -> n k", k=KEY_LOAD)
                with pool.Fori(0, E // KEY_LOAD) as n:
                    pool.wait_ge(keys_used, n * (KEY_LOAD // PAIR_KEYS) + 1)
                    pool.dma_start(bias[0:EP, 0:KEY_LOAD], spread[bass.ds(n, 1), :].broadcast_to([EP, KEY_LOAD])
                                   ).then_inc(keys_in, 16)
            clear(adj_in, cleared_in)
            scatter(adj_in, cleared_in, idx_in, 0)
            clear(adj_out, cleared_out)
            scatter(adj_out, cleared_out, idx_out, 1)

        @block.scalar
        def _(act):
            def turn_hi(l, t, s):
                act.wait_ge(xt_turned, l * NT + t + 1)
                nc.scalar.activation(xt_hi[:, s, :], turned[:, :], ACT.Copy).then_inc(xt_hi_done, 1)

            def split_hi(l, c, s):
                if l == LIN[GCN_LIN]:
                    act.wait_ge(wt_turned, c + 1)
                    nc.scalar.activation(turned_part(w_hi, c), turned[:, :].rearrange("p (k o) -> p k o", k=KD), ACT.Copy
                                         ).then_inc(w_hi_done, 1)
                    return
                act.wait_ge(raw_full[s], 16 * ((l * KD + c) // SLOTS + 1) if isinstance(c, int)
                            else 8 * (l * KD + c - s) + 16)
                if l == LIN[NEIGH1]:
                    act.wait_ge(acc_full, (SELF0 + 1) * NT)
                elif l > 0 and c < KD - 1:
                    act.wait_ge(w_used, (l * PAIRS - 1) * (KD - 1) + c + 1)
                elif l > 0:
                    act.wait_ge(acc_full, {LIN[SELF0]: SELF0, LIN[SELF1]: SELF1}[l] * NT)
                nc.scalar.activation(row(w_hi, c), raw[:, s, :], ACT.Copy).then_inc(w_hi_done, 1)

            def store(q, t, s):
                if q == SELF0:
                    act.wait_ge(acc_free, SLOTS + q * NT + t + 1)
                elif q == SELF1:
                    act.wait_ge(res_done, t + 1)
                elif q == MEAN0:
                    act.wait_ge(relu_done, t + 1)
                else:
                    act.wait_ge(norm_done, (0 if q == MEAN1 else NT) + t + 1)
                n = rows(t) if q == GCN_AGG else P
                act.dma_start(results[q][bass.ds(t * P, n), :], outb[0:n, s, :]).then_inc(stored[s], 16)

            def evict(q, t, s):
                if q in (NEIGH0, NEIGH1):
                    act.wait_ge(acc_full, q * NT + t + 1)
                    nc.scalar.activation(row(u_hi, t), acc[:, s, :], ACT.Copy).then_inc(u_hi_done, 1)
                elif q == GCN_LIN:
                    act.wait_ge(acc_free, SLOTS + q * NT + t + 1)
                    nc.scalar.activation(row(u_hi, t), outb[:, s, :], ACT.Copy, scale=dscale[:, bass.ds(t, 1)]
                                         ).then_inc(u_hi_done, 1)
                else:
                    if q in (MEAN1, GCN_AGG):
                        act.wait_ge(mv_done, (0 if q == MEAN1 else NT) + t + 1)
                        nc.scalar.activation(std[:, s:s + 1], mv[:, s, 1:2], ACT.Sqrt, bias=eps[:, 0:1]).then_inc(std_done, 1)
                    store(q, t, s)

            act.wait_ge(eps_ready, 1)
            turn_hi(0, 0, 0)
            for c in range(KD):
                split_hi(0, c, c % SLOTS)
            for q in range(8):
                def body(t, pair, s, chunk, q=q):
                    if q in LIN and not (isinstance(t, int) and t == NT - 1):
                        turn_hi(LIN[q], t + 1, 1 - s)
                    elif isinstance(t, int) and t == NT - 1 and q + 1 in LIN:
                        turn_hi(LIN[q + 1], 0, 0)
                        if q in LIN:
                            for c in range(KD):
                                split_hi(LIN[q + 1], c, c % SLOTS)
                    evict(q, t, s)
                    if q in AGG and q + 1 in LIN and chunk is not None:
                        split_hi(LIN[q + 1], chunk, s)
                tiles(act, body)
                if q == MEAN0:
                    act.wait_ge(dsum_done, NT)
                    nc.scalar.activation(dsqrt[:, :], dsum[:, :], ACT.Sqrt, bias=1.0).then_inc(dsqrt_done, 1)

        @block.vector
        def _(dve):
            def turn_lo(l, t, s):
                dve.wait_ge(xt_hi_done, l * NT + t + 1)
                nc.vector.tensor_tensor(xt_lo[:, s, :], turned[:, :], xt_hi[:, s, :].bitcast(F32), ALU.subtract
                                        ).then_inc(xt_lo_done, 1)

            def split_lo(l, c, s):
                dve.wait_ge(w_hi_done, l * KD + c + 1)
                if l == LIN[GCN_LIN]:
                    nc.vector.tensor_tensor(turned_part(w_lo, c), turned[:, :].rearrange("p (k o) -> p k o", k=KD),
                                            turned_part(w_hi, c).bitcast(F32), ALU.subtract).then_inc(w_lo_done, 1)
                else:
                    nc.vector.tensor_tensor(row(w_lo, c), raw[:, s, :], row(w_hi, c).bitcast(F32), ALU.subtract
                                            ).then_inc(w_lo_done, 1)

            def edge_list():
                steps = [0]

                def then_next(ins):
                    steps[0] += 1
                    ins.then_inc(prep, 1)
                    dve.wait_ge(prep, steps[0])

                dve.wait_ge(edges_in, 16 * 6)
                own = slice(WINDOW, WINDOW + EC)
                dst_hi, dst_lo, src_hi, src_lo = (p[0:EP, :] for p in part)
                nc.vector.scalar_tensor_tensor(key[0:EP, :], e_dst[0:EP, :], float(KEY_SHIFT), e_src[0:EP, :],
                                               ALU.mult, ALU.add)
                falls, long = (v[0:EP, :] for v in sums)
                nc.vector.tensor_tensor(falls, e_dst[0:EP, WINDOW + 1:WINDOW + 1 + EC], e_dst[0:EP, own], ALU.is_lt)
                then_next(nc.vector.tensor_tensor(long, e_dst[0:EP, 2 * WINDOW:2 * WINDOW + EC], e_dst[0:EP, own], ALU.is_le))
                then_next(nc.vector.tensor_tensor(falls, falls, long, ALU.add))
                nc.vector.tensor_reduce(bad[0:EP, 0:1], falls, AX_X, ALU.add).then_inc(bad_ready, 1)
                for ids, hi, lo in ((e_dst, dst_hi, dst_lo), (e_src, src_hi, src_lo)):
                    nc.vector.tensor_scalar(hi, ids[0:EP, own], 7, None, ALU.logical_shift_right)
                    then_next(nc.vector.tensor_scalar(lo, ids[0:EP, own], P - 1, None, ALU.bitwise_and))
                for index, r_hi, r_lo, s_hi, s_lo in ((idx_in, dst_hi, dst_lo, src_hi, src_lo),
                                                      (idx_out, src_hi, src_lo, dst_hi, dst_lo)):
                    at = index[0:EP, :]
                    then_next(nc.vector.scalar_tensor_tensor(at, s_hi, float(P), r_lo, ALU.mult, ALU.add))
                    then_next(nc.vector.scalar_tensor_tensor(at, s_lo, float(BLOCK), at, ALU.mult, ALU.add))
                    then_next(nc.vector.scalar_tensor_tensor(at, r_hi, float(P * BLOCK), at, ALU.mult, ALU.add))
                dve.wait_ge(bad_summed, 1)
                nc.vector.tensor_scalar(flag[0:1, 0:1], count[0:1, 0, 0:1], 0.0, None, ALU.is_gt).then_inc(flag_ready, 1)
                dve.wait_ge(flag_ready, 1)
                general = dve.value_load(flag[0:1, 0:1], min_val=0, max_val=1)
                with dve.If(general > 0):
                    with dve.Fori(0, E // KEY_LOAD) as n:
                        with dve.Fori(0, KEY_LOAD // PAIR_KEYS) as m:
                            c = n * (KEY_LOAD // PAIR_KEYS) + m
                            eq = adj[0:EP, 1, :].rearrange("p (e k) -> p e k", k=PAIR_KEYS)
                            mine = key[0:EP, own].unsqueeze(2).broadcast_to([EP, EC, PAIR_KEYS])
                            all_of = bias[0:EP, bass.ds(m * PAIR_KEYS, PAIR_KEYS)].unsqueeze(1).broadcast_to([EP, EC, PAIR_KEYS])
                            dve.wait_ge(keys_in, (n + 1) * 16)
                            nc.vector.tensor_tensor(eq, mine, all_of, ALU.is_equal).then_inc(keys_used, 1)
                            dve.wait_ge(keys_used, c + 2)
                            nc.vector.tensor_reduce(sums[0][0:EP, :], eq.bitcast(F32), AX_X, ALU.add).then_inc(pair_eq, 1)
                            dve.wait_ge(pair_eq, c + 1)
                            nc.vector.tensor_tensor(pairs[0:EP, :], pairs[0:EP, :], sums[0][0:EP, :], ALU.add).then_inc(pair_sum, 1)
                            dve.wait_ge(pair_sum, c + 1)
                nc.vector.memset(bad[0:EP, 1:2], 0.0).then_inc(flag_ready, 1)

            def repeats(b):
                STEPS = 8
                cols = bass.ds(b * BATCH, BATCH)
                before, behind, times, skip = (repeat[0:EP, k, :] for k in range(4))
                eq = adj[0:EP, 1, 0:BATCH * WINDOW].rearrange("p (c w) -> p c w", w=WINDOW)
                own = key[0:EP, bass.ds(b * BATCH + WINDOW, BATCH)].unsqueeze(2).broadcast_to([EP, BATCH, WINDOW])
                for k, (first, found) in enumerate(((0, before), (WINDOW + 1, behind))):
                    near = windows(key[0:EP, bass.ds(b * BATCH + first, BATCH)])
                    nc.vector.tensor_tensor(eq, own, near, ALU.is_equal).then_inc(same, 1)
                    dve.wait_ge(same, b * STEPS + 2 * k + 1)
                    nc.vector.tensor_reduce(found, eq.bitcast(F32), AX_X, ALU.add).then_inc(same, 1)
                    dve.wait_ge(same, b * STEPS + 2 * k + 2)
                nc.vector.scalar_tensor_tensor(times, before, 1.0, behind, ALU.add, ALU.add).then_inc(same, 1)
                nc.vector.tensor_scalar(skip, before, 0.0, float(SKIP), ALU.is_gt, ALU.mult).then_inc(same, 1)
                dve.wait_ge(same, b * STEPS + 6)
                nc.vector.tensor_tensor(mult[0:EP, cols], times, pairs[0:EP, cols], ALU.max).then_inc(same, 1)
                nc.vector.tensor_tensor(idx_out[0:EP, cols], idx_out[0:EP, cols], skip, ALU.add).then_inc(same, 1)
                dve.wait_ge(same, b * STEPS + 8)
                nc.vector.tensor_tensor(idx_in[0:EP, cols], idx_in[0:EP, cols], skip, ALU.add).then_inc(batch_ready, 1)
                dve.wait_ge(batch_ready, b + 1)

            def windows(ap):
                return bass.AP(tensor=ap.tensor, offset=ap.offset, ap=[*ap.ap, [1, WINDOW]])

            def degrees(t, s):
                nc.vector.tensor_scalar(degc[:, s:s + 1], count[:, s, 0:1], 1.0, None, ALU.max).then_inc(deg_step, 1)
                dve.wait_ge(deg_step, 2 * t + 1)
                nc.vector.reciprocal(dinv[:, bass.ds(t, 1)], degc[:, s:s + 1]).then_inc(deg_step, 1)
                nc.vector.tensor_reduce(dpart[:, s, :], adj[:, s, :].bitcast(F32).rearrange("p (a r) -> p a r", r=P), AX_X, ALU.add
                                        ).then_inc(dsum_part, 1)
                dve.wait_ge(dsum_part, t + 1)
                nc.vector.tensor_tensor(dsum[:, :], dsum[:, :], dpart[:, s, :], ALU.add).then_inc(dsum_done, 1)
                dve.wait_ge(dsum_done, t + 1)
                dve.wait_ge(deg_step, 2 * t + 2)

            def norm(q, t, s):
                n = (0 if q == MEAN1 else NT) + t + 1
                for c in range(NC):
                    nc.vector.bn_stats(stats[:, s, c, :], outb[:, s, c * PSUM_COLS:(c + 1) * PSUM_COLS]).then_inc(stats_done, 1)
                dve.wait_ge(stats_done, n * NC)
                nc.vector.memset(scrap_dve[:, :], 0.0)
                nc.vector.bn_aggr(mv[:, s, :], stats[:, s, :, :]).then_inc(mv_done, 1)
                dve.wait_ge(std_done, n)
                nc.vector.reciprocal(rstd[:, s:s + 1], std[:, s:s + 1]).then_inc(rstd_done, 1)
                dve.wait_ge(rstd_done, n)
                nc.vector.tensor_scalar(outb[:, s, :], outb[:, s, :], mv[:, s, 0:1], rstd[:, s:s + 1], ALU.subtract, ALU.mult
                                        ).then_inc(norm_done, 1)

            def evict(q, t, pair, s):
                z = outb[:, s, :]
                if q in (NEIGH0, NEIGH1):
                    dve.wait_ge(u_hi_done, (0 if q == NEIGH0 else NT) + t + 1)
                    nc.vector.tensor_tensor(row(u_lo, t), acc[:, s, :], row(u_hi, t).bitcast(F32), ALU.subtract).then_inc(acc_free, 1)
                    return
                dve.wait_ge(acc_full, q * NT + t + 1)
                if q in STORE:
                    dve.wait_ge(stored[s], 16 * (STORE[q] * PAIRS + pair + 1))
                elif q == GCN_LIN:
                    dve.wait_ge(stored[s], 16 * ((STORE[MEAN1] + 1) * PAIRS + 1))
                if q in biases:
                    dve.wait_ge(bias_full, 16 * (list(biases).index(q) + 1))
                    nc.vector.tensor_tensor(z, acc[:, s, :], bias[:, :], ALU.add).then_inc(acc_free, 1)
                if q == SELF1:
                    dve.wait_ge(acc_free, SLOTS + q * NT + t + 1)
                    dve.wait_ge(raw_full[s], 16 * ((LIN[SELF1] + 1) * KD // SLOTS + pair + 1))
                    nc.vector.tensor_tensor(z, z, raw[:, s, :], ALU.add).then_inc(res_done, 1)
                elif q == GCN_LIN:
                    dve.wait_ge(u_hi_done, 2 * NT + t + 1)
                    nc.vector.scalar_tensor_tensor(row(u_lo, t), z, dscale[:, bass.ds(t, 1)], row(u_hi, t).bitcast(F32),
                                                   ALU.mult, ALU.subtract).then_inc(u_lo_done, 1)
                elif q in (MEAN0, MEAN1):
                    if q == MEAN0:
                        degrees(t, s)
                    dve.wait_ge(xin_full[s], 16 * (q * PAIRS + pair + 1))
                    nc.vector.scalar_tensor_tensor(z, acc[:, s, :], dinv[:, bass.ds(t, 1)], xin[:, s, :], ALU.mult, ALU.add
                                                   ).then_inc(acc_free, 1)
                    dve.wait_ge(acc_free, SLOTS + q * NT + t + 1)
                    if q == MEAN0:
                        nc.vector.tensor_scalar(z, z, 0.0, None, ALU.max).then_inc(relu_done, 1)
                    else:
                        norm(q, t, s)
                elif q == GCN_AGG:
                    nc.vector.tensor_tensor(z, acc[:, s, :], row(u_hi, t).bitcast(F32), ALU.add).then_inc(acc_free, 1)
                    dve.wait_ge(acc_free, SLOTS + q * NT + t + 1)
                    nc.vector.tensor_tensor(z, z, row(u_lo, t).bitcast(F32), ALU.add).then_inc(loop_added, 1)
                    dve.wait_ge(loop_added, t + 1)
                    dve.wait_ge(xin_full[s], 16 * (q * PAIRS + pair + 1))
                    nc.vector.scalar_tensor_tensor(z, z, dscale[:, bass.ds(t, 1)], xin[:, s, :], ALU.mult, ALU.add).then_inc(z_done, 1)
                    dve.wait_ge(z_done, t + 1)
                    norm(q, t, s)

            nc.vector.memset(eps[:, :], EPS).then_inc(eps_ready, 1)
            nc.vector.memset(ones[:, :].bitcast(F32), 1.0).then_inc(ones_ready, 1)
            nc.vector.memset(ones_f[:, :], 1.0).then_inc(ones_ready, 1)
            nc.vector.memset(dsum[:, :], 0.0).then_inc(dsum_zero, 1)
            nc.vector.memset(pairs[:, :], 0.0).then_inc(keys_used, 1)
            for s in range(SLOTS):
                nc.vector.memset(degc[:, s:s + 1], 0.0).then_inc(acc_free, 1)
                nc.vector.memset(std[:, s:s + 1], 0.0).then_inc(stored[s], 16)
            dve.wait_ge(dsum_zero, 1)
            dve.wait_ge(keys_used, 1)
            turn_lo(0, 0, 0)
            for c in range(KD):
                split_lo(0, c, c % SLOTS)
            edge_list()
            for q in range(8):
                def body(t, pair, s, chunk, q=q):
                    if q in LIN and not (isinstance(t, int) and t == NT - 1):
                        turn_lo(LIN[q], t + 1, 1 - s)
                    elif isinstance(t, int) and t == NT - 1 and q + 1 in LIN:
                        turn_lo(LIN[q + 1], 0, 0)
                        if q in LIN:
                            for c in range(KD):
                                split_lo(LIN[q + 1], c, c % SLOTS)
                    if q == NEIGH0:
                        repeats(t)
                    evict(q, t, pair, s)
                    if q in AGG and q + 1 in LIN and chunk is not None:
                        split_lo(LIN[q + 1], chunk, s)
                tiles(dve, body)
                if q == MEAN0:
                    dve.wait_ge(dsqrt_done, 1)
                    nc.vector.reciprocal(dscale[:, :], dsqrt[:, :]).then_inc(dscale_done, 1)
                    dve.wait_ge(dscale_done, 1)

        @block.tensor
        def _(pe):
            def turn_tile(q, t, pair, s):
                pe.wait_ge(xin_full[s], 16 * (q * PAIRS + pair + 1))
                for k in range(KD):
                    ins = nc.tensor.transpose(turned[:, k * P:(k + 1) * P], xin[:, s, k * P:(k + 1) * P], ident[:, :])
                ins.then_inc(xt_turned, 1)

            def turn_weights(c, s):
                pe.wait_ge(raw_full[s], 8 * (LIN[GCN_LIN] * KD + c - s) + 16 * (PAIRS + 1))
                pe.wait_ge(w_lo_done, LIN[GCN_LIN] * KD + c)
                for k in range(KD):
                    ins = nc.tensor.transpose(turned[:, k * P:(k + 1) * P], raw[:, s, k * P:(k + 1) * P], ident[:, :])
                ins.then_inc(wt_turned, 1)

            def linear(q, t, pair, s):
                l = LIN[q]
                last = isinstance(t, int) and t == NT - 1
                pe.wait_ge(xt_lo_done, l * NT + t + 1)
                pe.wait_ge(acc_free, q * NT + t + 1)
                for k in range(KD):
                    if k == KD // 2:
                        if not last:
                            turn_tile(q, t + 1, pair + s, 1 - s)
                        elif q + 1 in LIN:
                            turn_tile(q + 1, 0, 0, 0)
                    if s == 0:
                        pe.wait_ge(w_lo_done, l * KD + (k + 1 if l != LIN[GCN_LIN] else KD))
                    left = [part[:, s, k * P:(k + 1) * P] for part in (xt_hi, xt_lo)]
                    for a, right in ((left[0], w_hi), (left[0], w_lo), (left[1], w_hi)):
                        for n in range(NC):
                            cols = slice(n * PSUM_COLS, (n + 1) * PSUM_COLS)
                            ins = nc.tensor.matmul(acc[:, s, cols], a, right[:, k, cols], start=(k == 0 and right is w_hi and a is left[0]),
                                                   stop=(k == KD - 1 and a is left[1]))
                    if k == KD - 1:
                        ins.then_inc(acc_full, 1)
                    elif s == SLOTS - 1:
                        ins.then_inc(w_used, 1)

            def aggregate(q, t, pair, s, chunk, exact):
                def typed(ap):
                    return ap.bitcast(F32) if exact else ap
                pe.wait_ge(acc_free, q * NT + t + 1)
                pe.wait_ge(adj_full[s], 16 * (AGG[q] * PAIRS + pair + 1))
                if isinstance(t, int) and t == NT - 1 and q + 1 in LIN:
                    if q == MEAN1:
                        pe.wait_ge(w_lo_done, (LIN[GCN_LIN] + 1) * KD)
                    turn_tile(q + 1, 0, 0, 0)
                for k in range(NT):
                    n_k = rows(k)
                    a = typed(adj[0:n_k, s, k * P:(k + 1) * P])
                    if q == MEAN0:
                        nc.tensor.matmul(count[:, s, 0:2], a, typed(ones[0:n_k, :]), start=(k == 0), stop=(k == NT - 1))
                    for part in (u_hi, u_lo):
                        for n in range(NC):
                            cols = slice(n * PSUM_COLS, (n + 1) * PSUM_COLS)
                            ins = nc.tensor.matmul(acc[:, s, cols], a, typed(part[0:n_k, k, cols]),
                                                   start=(k == 0 and part is u_hi), stop=(k == NT - 1 and part is u_lo))
                ins.then_inc(acc_full, 1)
                if q == MEAN1 and chunk is not None:
                    turn_weights(chunk, s)

            pe.wait_ge(ident_ready, 1)
            pe.wait_ge(ones_ready, 2)
            turn_tile(NEIGH0, 0, 0, 0)
            pe.wait_ge(bad_ready, 1)
            nc.tensor.matmul(count[0:1, 0, 0:1], bad[0:EP, 0:1], ones_f[0:EP, :], start=True, stop=True).then_inc(bad_summed, 1)
            for q in range(8):
                if q in LIN:
                    tiles(pe, lambda t, pair, s, chunk, q=q: linear(q, t, pair, s))
                    continue
                if q == MEAN0:
                    pe.wait_ge(flag_ready, 2)
                    general = pe.value_load(flag[0:1, 0:1], min_val=0, max_val=1)
                if q == GCN_AGG:
                    pe.wait_ge(u_lo_done, NT)
                with pe.If(general > 0):
                    tiles(pe, lambda t, pair, s, chunk, q=q: aggregate(q, t, pair, s, chunk, True))
                with pe.Else():
                    tiles(pe, lambda t, pair, s, chunk, q=q: aggregate(q, t, pair, s, chunk, False))


_INS = ["x", "src", "dst", "L0_gnn_W_self0", "L0_gnn_W_neigh0", "L0_gnn_b0", "L0_gnn_W_self1", "L0_gnn_W_neigh1", "L0_gnn_b1",
        "L1_gnn_W", "L1_gnn_b"]


def kernel(**inputs):
    import numpy as _np
    import concourse.bacc as _bacc
    from concourse import mybir as _mybir
    from concourse.bass_utils import run_bass_kernel_spmd as _run

    nc = _bacc.Bacc("TRN2", target_bir_lowering=False, num_devices=1)
    arrays, args = {}, []
    for name in _INS:
        a = _np.ascontiguousarray(inputs[name])
        arrays[f"in_{name}"] = a
        args.append(nc.dram_tensor(f"in_{name}", a.shape, _mybir.dt.from_np(a.dtype), kind="ExternalInput").ap())
    shape = inputs["x"].shape
    args.append(nc.dram_tensor("out", shape, _mybir.dt.float32, kind="ExternalOutput").ap())
    build(nc, *args)
    r = _run(nc, [arrays], core_ids=[0])
    return r.results[0]["out"]
```

```python
from contextlib import ExitStack

import concourse.bass as bass
from concourse import mybir

P = 128
PSUM_COLS = 512
WINDOW = 48
NO_NODE = 4095
SKIP = 1 << 22
KEY_SHIFT = 2048
EPS = 1e-5

F32 = mybir.dt.float32
F32R = mybir.dt.float32r
I32 = mybir.dt.int32
ACT = mybir.ActivationFunctionType
ALU = mybir.AluOpType
AX_X = mybir.AxisListType.X


def build(nc, x, src, dst, w_self0, w_neigh0, b0, w_self1, w_neigh1, b1, w_gcn, b_gcn, out):
    N, D = x.shape
    E = src.shape[0]
    NT = -(-N // P)
    LAST = N - (NT - 1) * P
    KD = D // P
    NC = D // PSUM_COLS
    EP = 125
    EC = E // EP
    BATCH = EC // NT
    SLOTS = 2
    PAIRS = NT // SLOTS
    BLOCK = NT * P
    CELLS = NT * P * BLOCK
    HALO = EC + 2 * WINDOW
    PAIR_KEYS = BLOCK // EC
    ZEROS = 2 * P
    KEY_LOAD = 1000
    assert E == EP * EC and EC % NT == 0 and NT % SLOTS == 0 and KD % SLOTS == 0
    assert E % KEY_LOAD == 0 and KEY_LOAD % PAIR_KEYS == 0 and KEY_LOAD <= D
    assert BATCH * WINDOW <= BLOCK and N < KEY_SHIFT - 1 and SKIP > CELLS

    NEIGH0, SELF0, MEAN0, NEIGH1, SELF1, MEAN1, GCN_LIN, GCN_AGG = range(8)
    LIN = {NEIGH0: 0, SELF0: 1, NEIGH1: 2, SELF1: 3, GCN_LIN: 4}
    AGG = {MEAN0: 0, MEAN1: 1, GCN_AGG: 2}
    TURN = {NEIGH0: 0, NEIGH1: 1, GCN_LIN: 2}
    XIN = {NEIGH0: 0, MEAN0: 1, NEIGH1: 2, SELF1: 3, MEAN1: 4, GCN_LIN: 5, GCN_AGG: 6}
    STORE = {SELF0: 0, MEAN0: 1, SELF1: 2, MEAN1: 3, GCN_AGG: 4}

    with ExitStack() as ctx:
        def sb(name, shape, dt):
            return ctx.enter_context(nc.sbuf_tensor(name, shape, dt))

        def sem(name):
            return ctx.enter_context(nc.semaphore(name))

        def dram(name, shape, dt=F32):
            return nc.dram_tensor(name, shape, dt, kind="Internal").ap()

        self_scr = dram("self_scr", [NT * P, D])
        h_scr = dram("h_scr", [NT * P, D])
        y_scr = dram("y_scr", [NT * P, D])
        xt_hi_scr = dram("xt_hi_scr", [NT * P, D])
        xt_lo_scr = dram("xt_lo_scr", [NT * P, D])
        keys_scr = dram("keys_scr", [E])
        adj_in = dram("adj_in", [CELLS, 1])
        adj_out = dram("adj_out", [CELLS, 1])

        u_hi = sb("u_hi", [P, NT, D], F32R)
        u_lo = sb("u_lo", [P, NT, D], F32R)
        w_hi = sb("w_hi", [P, KD, D], F32R)
        w_lo = sb("w_lo", [P, KD, D], F32R)
        xt_hi = sb("xt_hi", [P, SLOTS, D], F32R)
        xt_lo = sb("xt_lo", [P, SLOTS, D], F32R)
        adj = sb("adj", [P, SLOTS, BLOCK], F32R)
        ones = sb("ones", [P, 2], F32R)

        xin = sb("xin", [P, SLOTS, D], F32)
        raw = sb("raw", [P, SLOTS, D], F32)
        outb = sb("outb", [P, SLOTS, D], F32)
        bias = sb("bias", [P, D], F32)
        zeros = sb("zeros", [P, ZEROS], F32)
        ident = sb("ident", [P, P], F32)
        key = sb("key", [P, HALO], F32)
        idx_in = sb("idx_in", [P, EC], I32)
        idx_out = sb("idx_out", [P, EC], I32)
        mult = sb("mult", [P, EC], F32)
        loops = sb("loops", [P, EC], F32)
        ones_nt = sb("ones_nt", [P, NT], F32)
        pairs = sb("pairs", [P, EC], F32)
        repeat = sb("repeat", [P, 4, BATCH], F32)
        idx_slot = sb("idx_slot", [P, SLOTS, BATCH], I32)
        mult_slot = sb("mult_slot", [P, SLOTS, BATCH], F32)
        bad = sb("bad", [P, 4], F32)
        flag = sb("flag", [P, 2], I32)
        dinv = sb("dinv", [P, NT], F32)
        degc = sb("degc", [P, SLOTS], F32)
        dsum = sb("dsum", [P, NT], F32)
        dpart = sb("dpart", [P, SLOTS, NT], F32)
        dsqrt = sb("dsqrt", [P, NT], F32)
        dscale = sb("dscale", [P, NT], F32)
        stats = sb("stats", [P, SLOTS, NC, 6], F32)
        mv = sb("mv", [P, SLOTS, 2], F32)
        std = sb("std", [P, SLOTS], F32)
        var = sb("var", [P, SLOTS], F32)
        rstd = sb("rstd", [P, SLOTS], F32)
        eps = sb("eps", [P, 1], F32)
        scrap_dve = sb("scrap_dve", [P, 1], F32)
        scrap_pool = sb("scrap_pool", [P, 1], F32)
        ones_f = sb("ones_f", [P, 1], F32)

        e_dst = bias[:, 0:HALO].bitcast(I32)
        e_src = bias[:, HALO:2 * HALO].bitcast(I32)
        e_part = [*(bias[:, 2 * HALO + i * EC:2 * HALO + (i + 1) * EC].bitcast(I32) for i in range(3)), mult[:, :].bitcast(I32)]
        falls, long = (idx[:, :].bitcast(F32) for idx in (idx_in, idx_out))
        assert 2 * HALO + 3 * EC <= D

        raw_slots = [raw[:, 0, :], raw[:, 1, :], outb[:, 0, :], outb[:, 1, :]]

        acc = ctx.enter_context(nc.psum_tensor("acc", [P, SLOTS, D], F32))
        turned = ctx.enter_context(nc.psum_tensor("turned", [P, D], F32))
        count = ctx.enter_context(nc.psum_tensor("count", [P, SLOTS, PSUM_COLS], F32))

        edges_in = sem("edges_in")
        halo_set = sem("halo_set")
        ident_zero = sem("ident_zero")
        ident_ready = sem("ident_ready")
        ones_ready = sem("ones_ready")
        zeros_ready = sem("zeros_ready")
        cleared_in = sem("cleared_in")
        cleared_out = sem("cleared_out")
        diagonal_set = sem("diagonal_set")
        prep = sem("prep")
        bad_ready = sem("bad_ready")
        bad_summed = sem("bad_summed")
        flag_ready = sem("flag_ready")
        keys_out = sem("keys_out")
        keys_in = sem("keys_in")
        keys_used = sem("keys_used")
        pair_eq = sem("pair_eq")
        pair_sum = sem("pair_sum")
        same = sem("same")
        batch_ready = sem("batch_ready")
        batch_copied = sem("batch_copied")
        scattered = [sem(f"scattered{s}") for s in range(SLOTS)]
        wt_turned = sem("wt_turned")
        xin_full = [sem(f"xin_full{s}") for s in range(SLOTS)]
        raw_full = [sem(f"raw_full{s}") for s in range(2 * SLOTS)]
        xt_stored = [sem(f"xt_stored{s}") for s in range(SLOTS)]
        xt_full = [sem(f"xt_full{s}") for s in range(SLOTS)]
        adj_full = [sem(f"adj_full{s}") for s in range(SLOTS)]
        stored = [sem(f"stored{s}") for s in range(SLOTS)]
        bias_full = sem("bias_full")
        xt_turned = sem("xt_turned")
        xt_hi_done = sem("xt_hi_done")
        xt_lo_done = sem("xt_lo_done")
        w_hi_done = sem("w_hi_done")
        w_lo_done = sem("w_lo_done")
        w_used = sem("w_used")
        acc_full = sem("acc_full")
        acc_free = sem("acc_free")
        u_hi_done = sem("u_hi_done")
        u_lo_done = sem("u_lo_done")
        res_done = sem("res_done")
        deg_step = sem("deg_step")
        dsum_zero = sem("dsum_zero")
        dsum_part = sem("dsum_part")
        dsum_done = sem("dsum_done")
        dsqrt_done = sem("dsqrt_done")
        dscale_step = sem("dscale_step")
        relu_done = sem("relu_done")
        stats_done = sem("stats_done")
        mv_done = sem("mv_done")
        std_done = sem("std_done")
        rstd_step = sem("rstd_step")
        norm_done = sem("norm_done")
        eps_ready = sem("eps_ready")

        sources = {NEIGH0: x, MEAN0: self_scr, NEIGH1: h_scr, SELF1: x, MEAN1: self_scr, GCN_LIN: y_scr, GCN_AGG: y_scr}
        made_by = {MEAN0: SELF0, NEIGH1: MEAN0, MEAN1: SELF1, GCN_LIN: MEAN1, GCN_AGG: MEAN1}
        results = {SELF0: self_scr, MEAN0: h_scr, SELF1: self_scr, MEAN1: y_scr, GCN_AGG: out}
        weights = [w_neigh0, w_self0, w_neigh1, w_self1, w_gcn]
        biases = {SELF0: b0, SELF1: b1, GCN_LIN: b_gcn}

        def rows(t):
            return LAST if isinstance(t, int) and t == NT - 1 else P

        def tiles(eng, body):
            with eng.Fori(0, PAIRS - 1) as i:
                for s in range(SLOTS):
                    body(i * SLOTS + s, i, s, i * SLOTS + s)
            for s in range(SLOTS):
                body(NT - SLOTS + s, PAIRS - 1, s, None)

        def raw_slot(l, c):
            return c % (2 * SLOTS) if l in (LIN[NEIGH0], LIN[SELF0], LIN[SELF1]) else c % SLOTS

        def raw_count(l, c):
            before = sum(raw_slot(m, d) == raw_slot(l, c) for m in range(l) for d in range(KD))
            return before + sum(raw_slot(l, d) == raw_slot(l, c) for d in range(c + 1))

        def raw_wait(l, c, s):
            if isinstance(c, int):
                return 16 * raw_count(l, c)
            return 16 * raw_count(l, s) + 8 * (c - s)

        def row(buf, t):
            return buf[:, bass.ds(t, 1), :].rearrange("p a d -> p (a d)")

        def turned_part(buf, c):
            return buf[:, :, bass.ds(c * P, P)]

        block = ctx.enter_context(nc.Block())

        @block.sync
        def _(sp):
            def load_weights(l, c, s):
                if not isinstance(c, int):
                    sp.wait_ge(w_lo_done, l * KD + c - SLOTS + 1)
                elif raw_slot(l, c) >= SLOTS and c < 2 * SLOTS:
                    if l == LIN[SELF0]:
                        sp.wait_ge(w_lo_done, LIN[SELF0] * KD)
                    elif l == LIN[SELF1]:
                        sp.wait_ge(stored[s % SLOTS], 16 * ((STORE[MEAN0] + 1) * PAIRS + 1))
                elif raw_count(l, c) > 1:
                    chunks = [m * KD + d for m in range(l + 1) for d in range(KD)
                              if m * KD + d < l * KD + c and raw_slot(m, d) == raw_slot(l, c)]
                    sp.wait_ge(w_lo_done, chunks[-1] + 1)
                slot = s if not isinstance(c, int) else raw_slot(l, c)
                sp.dma_start(raw_slots[slot], weights[l][bass.ds(c * P, P), :]).then_inc(raw_full[slot], 16)

            def load_tile(q, t, pair, s):
                before, t_before = q, t - SLOTS
                if isinstance(t, int) and t < SLOTS:
                    before = next((p for p in XIN if XIN[p] == XIN[q] - 1), None)
                    t_before = NT - SLOTS + s
                if before in TURN:
                    sp.wait_ge(xt_turned, TURN[before] * NT + t_before + 1)
                elif before == SELF1:
                    sp.wait_ge(res_done, t_before + 1)
                elif before in AGG:
                    sp.wait_ge(acc_free, SLOTS + before * NT + t_before + 1)
                if q in made_by:
                    sp.wait_ge(stored[s], 16 * (STORE[made_by[q]] * PAIRS + pair + 2))
                n = rows(t) if sources[q] is x else P
                sp.dma_start(xin[0:n, s, :], sources[q][bass.ds(t * P, n), :]).then_inc(xin_full[s], 16)

            def load_turned(q, t, s):
                sp.wait_ge(acc_full, q * NT + t - SLOTS + 1)
                if isinstance(t, int) and t < SLOTS:
                    for b in range(SLOTS):
                        sp.wait_ge(xt_stored[b], 16 + 32 * (TURN[q - 1] + 1) * PAIRS)
                for scr, buf in ((xt_hi_scr, xt_hi), (xt_lo_scr, xt_lo)):
                    sp.dma_start(buf[:, s, :].bitcast(F32), scr[bass.ds(t * P, P), :]).then_inc(xt_full[s], 16)

            def load_adj(q, t, s):
                if isinstance(t, int) and t < SLOTS and q != MEAN0:
                    sp.wait_ge(acc_full, ({MEAN1: MEAN0, GCN_AGG: MEAN1}[q] + 1) * NT)
                    sp.wait_ge(dsum_part, NT)
                table = (adj_out if q == GCN_AGG else adj_in).rearrange("(a p b) o -> a p (b o)", p=P, b=BLOCK)
                sp.dma_start(adj[:, s, :].bitcast(F32), table[bass.ds(t, 1), :, :].rearrange("a p b -> (a p) b")
                             ).then_inc(adj_full[s], 16)

            def load_bias(q):
                if q == SELF0:
                    sp.wait_ge(flag_ready, 2)
                else:
                    sp.wait_ge(acc_free, SLOTS + ({SELF1: SELF0, GCN_LIN: SELF1}[q] + 1) * NT)
                sp.dma_start(bias[:, :], biases[q].rearrange("(a d) -> a d", a=1).broadcast_to([P, D])).then_inc(bias_full, 16)

            def tile(q, t, pair, s):
                if q in XIN:
                    load_tile(q, t, pair, s)
                if q in (SELF0, SELF1):
                    load_turned(q, t, s)
                if q in AGG:
                    load_adj(q, t, s)
                    if q + 1 in LIN and not (isinstance(t, int) and t >= KD):
                        load_weights(LIN[q + 1], t, s)

            def other_tiles(q):
                with sp.Fori(1, PAIRS - 1) as i:
                    for s in range(SLOTS):
                        tile(q, i * SLOTS + s, i, s)
                for s in range(SLOTS):
                    tile(q, NT - SLOTS + s, PAIRS - 1, s)

            load_tile(NEIGH0, 0, 0, 0)
            for c in range(2 * SLOTS):
                load_weights(0, c, c)
            sp.wait_ge(halo_set, 2)
            for ids, where in ((dst, e_dst), (src, e_src)):
                grid = ids.rearrange("(p c) -> p c", c=EC)
                sp.dma_start(where[0:EP, WINDOW:WINDOW + EC], grid).then_inc(edges_in, 16)
                sp.dma_start(where[1:EP, 0:WINDOW], grid[0:EP - 1, EC - WINDOW:EC]).then_inc(edges_in, 16)
                sp.dma_start(where[0:EP - 1, WINDOW + EC:HALO], grid[1:EP, 0:WINDOW]).then_inc(edges_in, 16)
            for c in range(2 * SLOTS, KD):
                load_weights(0, c, c)
            load_tile(NEIGH0, 1, 0, 1)
            other_tiles(NEIGH0)
            for q in range(1, 8):
                if q in LIN and q - 1 in LIN:
                    for c in range(2 * SLOTS):
                        load_weights(LIN[q], c, c)
                    tile(q, 0, 0, 0)
                    for c in range(2 * SLOTS, KD):
                        load_weights(LIN[q], c, c)
                    tile(q, 1, 0, 1)
                else:
                    if q == MEAN0:
                        for s in range(SLOTS):
                            sp.wait_ge(scattered[s], 16 * EC // SLOTS)
                    if q == GCN_AGG:
                        for s in range(SLOTS):
                            sp.wait_ge(scattered[s], 16 * EC)
                    for s in range(SLOTS):
                        tile(q, s, 0, s)
                if q in biases:
                    load_bias(q)
                other_tiles(q)
            for s in range(SLOTS):
                sp.wait_ge(stored[s], 16 * ((STORE[GCN_AGG] + 1) * PAIRS + 1))

        @block.gpsimd
        def _(pool):
            nc.gpsimd.memset(e_dst[0:EP, :], NO_NODE).then_inc(halo_set, 1)
            nc.gpsimd.memset(e_src[0:EP, :], NO_NODE).then_inc(halo_set, 1)
            nc.gpsimd.memset(ident[:, :], 0.0).then_inc(ident_zero, 1)
            pool.wait_ge(ident_zero, 1)
            nc.gpsimd.affine_select(out=ident[:, :], in_=ident[:, :], compare_op=ALU.not_equal, fill=1.0, base=0,
                                    pattern=[[-1, P]], channel_multiplier=1).then_inc(ident_ready, 1)
            nc.gpsimd.memset(zeros[:, :], 0.0).then_inc(zeros_ready, 1)
            pool.wait_ge(zeros_ready, 1)

            def clear(table, done):
                blocks = table.rearrange("(a p b) o -> a p (b o)", p=P, b=BLOCK)
                for a in range(NT):
                    pool.dma_start(blocks[a].rearrange("p (c z) -> p c z", z=ZEROS), zeros[:, :].unsqueeze(1).broadcast_to([P, BLOCK // ZEROS, ZEROS])).then_inc(done, 16)

            def scatter(table, cleared, index, counts, scattered_before):
                def batch(i, s):
                    b = i * SLOTS + s
                    pool.wait_ge(batch_ready, b + 1)
                    if scattered_before or not isinstance(i, int):
                        pool.wait_ge(scattered[s], (i + scattered_before * PAIRS) * (16 * BATCH))
                    cols = bass.ds(b * BATCH, BATCH)
                    nc.gpsimd.tensor_copy(idx_slot[0:EP, s, :], index[0:EP, cols]).then_inc(batch_copied, 1)
                    nc.gpsimd.tensor_copy(mult_slot[0:EP, s, :], counts[0:EP, cols]).then_inc(batch_copied, 1)
                    pool.wait_ge(cleared, 16 * NT)
                    pool.wait_ge(batch_copied, (b + 1 + scattered_before * NT) * 2)
                    nc.gpsimd.tensor_tensor(scrap_pool[0:EP, :], mult_slot[0:EP, s, 0:1], mult_slot[0:EP, s, 0:1], ALU.add)
                    for j in range(BATCH):
                        pool.indirect_dma_start(
                            table, bass.IndirectOffsetOnAxis(ap=idx_slot[0:EP, s, j:j + 1], axis=0),
                            mult_slot[0:EP, s, j:j + 1], None, bounds_check=CELLS - 1, oob_is_err=False,
                        ).then_inc(scattered[s], 16)

                for s in range(SLOTS):
                    batch(0, s)
                with pool.Fori(1, PAIRS) as i:
                    for s in range(SLOTS):
                        batch(i, s)

            pool.wait_ge(ones_ready, 3)
            pool.wait_ge(raw_full[raw_slot(0, KD - 1)], raw_wait(0, KD - 1, 0))
            clear(adj_in, cleared_in)
            pool.wait_ge(flag_ready, 1)
            general = pool.value_load(flag[0:1, 0:1], min_val=0, max_val=1)
            with pool.If(general > 0):
                pool.dma_start(keys_scr.rearrange("(p c) -> p c", c=EC), key[0:EP, WINDOW:WINDOW + EC]).then_inc(keys_out, 16)
                pool.wait_ge(keys_out, 16)
                spread = keys_scr.rearrange("(n k) -> n k", k=KEY_LOAD)
                with pool.Fori(0, E // KEY_LOAD) as n:
                    pool.wait_ge(keys_used, n * (KEY_LOAD // PAIR_KEYS) + 1)
                    pool.dma_start(bias[0:EP, 0:KEY_LOAD], spread[bass.ds(n, 1), :].broadcast_to([EP, KEY_LOAD])
                                   ).then_inc(keys_in, 16)
            scatter(adj_in, cleared_in, idx_in, mult, 0)
            clear(adj_out, cleared_out)
            pool.wait_ge(cleared_out, 16 * NT)
            diagonal = bass.AP(tensor=adj_out.tensor, offset=0, ap=[[BLOCK + 1, P], [P * BLOCK + P, NT]])
            pool.dma_start(diagonal, ones_nt[:, :], allow_slow_non_contiguous=True).then_inc(diagonal_set, 16)
            pool.wait_ge(diagonal_set, 16)
            scatter(adj_out, cleared_out, idx_out, loops, 1)

        @block.scalar
        def _(act):
            def turn_hi(l, t, s):
                act.wait_ge(xt_turned, l * NT + t + 1)
                if l < TURN[GCN_LIN]:
                    act.wait_ge(xt_stored[s], 16 + 32 * l * PAIRS + 16 * (t - s))
                else:
                    act.wait_ge(xt_stored[s], 16 + 32 * TURN[GCN_LIN] * PAIRS)
                nc.scalar.activation(xt_hi[:, s, :], turned[:, :], ACT.Copy).then_inc(xt_hi_done, 1)

            def split_hi(l, c, s):
                if l == LIN[GCN_LIN]:
                    act.wait_ge(wt_turned, c + 1)
                    nc.scalar.activation(turned_part(w_hi, c), turned[:, :].rearrange("p (k o) -> p k o", k=KD), ACT.Copy
                                         ).then_inc(w_hi_done, 1)
                    return
                slot = raw_slot(l, c) if isinstance(c, int) else s
                act.wait_ge(raw_full[slot], raw_wait(l, c, s))
                if l == LIN[NEIGH1]:
                    act.wait_ge(acc_full, (SELF0 + 1) * NT)
                elif l > 0 and c < KD - 1:
                    act.wait_ge(w_used, (l * PAIRS - 1) * (KD - 1) + c + 1)
                elif l > 0:
                    act.wait_ge(acc_full, {LIN[SELF0]: SELF0, LIN[SELF1]: SELF1}[l] * NT)
                nc.scalar.activation(row(w_hi, c), raw_slots[slot], ACT.Copy).then_inc(w_hi_done, 1)

            def store_turned(l, t, s):
                act.wait_ge(xt_lo_done, l * NT + t + 1)
                for scr, buf in ((xt_hi_scr, xt_hi), (xt_lo_scr, xt_lo)):
                    act.dma_start(scr[bass.ds(t * P, P), :], buf[:, s, :].bitcast(F32)).then_inc(xt_stored[s], 16)

            def store(q, t, s):
                if q == SELF0:
                    act.wait_ge(acc_free, SLOTS + q * NT + t + 1)
                elif q == SELF1:
                    act.wait_ge(res_done, t + 1)
                elif q == MEAN0:
                    act.wait_ge(relu_done, t + 1)
                else:
                    act.wait_ge(norm_done, (0 if q == MEAN1 else NT) + t + 1)
                n = rows(t) if q == GCN_AGG else P
                act.dma_start(results[q][bass.ds(t * P, n), :], outb[0:n, s, :]).then_inc(stored[s], 16)

            def evict(q, t, s):
                if q in (NEIGH0, NEIGH1):
                    act.wait_ge(acc_full, q * NT + t + 1)
                    nc.scalar.activation(row(u_hi, t), acc[:, s, :], ACT.Copy).then_inc(u_hi_done, 1)
                elif q == GCN_LIN:
                    act.wait_ge(acc_free, SLOTS + q * NT + t + 1)
                    nc.scalar.activation(row(u_hi, t), outb[:, s, :], ACT.Copy, scale=dscale[:, bass.ds(t, 1)]
                                         ).then_inc(u_hi_done, 1)
                else:
                    if q in (MEAN1, GCN_AGG):
                        act.wait_ge(mv_done, (0 if q == MEAN1 else NT) + t + 1)
                        nc.scalar.activation(std[:, s:s + 1], mv[:, s, 1:2], ACT.Sqrt, bias=eps[:, 0:1]).then_inc(std_done, 1)
                    store(q, t, s)

            act.wait_ge(eps_ready, 1)
            turn_hi(0, 0, 0)
            for c in range(KD):
                split_hi(0, c, c)
            store_turned(0, 0, 0)
            for q in range(8):
                def body(t, pair, s, chunk, q=q):
                    last = isinstance(t, int) and t == NT - 1
                    if q in TURN and not last:
                        turn_hi(TURN[q], t + 1, 1 - s)
                    elif last and q + 1 in TURN:
                        turn_hi(TURN[q + 1], 0, 0)
                    elif last and q + 1 in LIN:
                        for c in range(KD):
                            split_hi(LIN[q + 1], c, c)
                    evict(q, t, s)
                    if q in (NEIGH0, NEIGH1) and not last:
                        store_turned(TURN[q], t + 1, 1 - s)
                    elif last and q + 1 == NEIGH1:
                        store_turned(TURN[q + 1], 0, 0)
                    if q in AGG and q + 1 in LIN and chunk is not None:
                        split_hi(LIN[q + 1], chunk, s)
                tiles(act, body)
                if q == MEAN0:
                    act.wait_ge(dscale_step, 1)
                    nc.scalar.activation(dsqrt[:, :], dsum[:, :], ACT.Sqrt).then_inc(dsqrt_done, 1)

        @block.vector
        def _(dve):
            def turn_lo(l, t, s):
                dve.wait_ge(xt_hi_done, l * NT + t + 1)
                nc.vector.tensor_tensor(xt_lo[:, s, :], turned[:, :], xt_hi[:, s, :].bitcast(F32), ALU.subtract
                                        ).then_inc(xt_lo_done, 1)

            def split_lo(l, c, s):
                dve.wait_ge(w_hi_done, l * KD + c + 1)
                if l == LIN[GCN_LIN]:
                    nc.vector.tensor_tensor(turned_part(w_lo, c), turned[:, :].rearrange("p (k o) -> p k o", k=KD),
                                            turned_part(w_hi, c).bitcast(F32), ALU.subtract).then_inc(w_lo_done, 1)
                else:
                    slot = raw_slot(l, c) if isinstance(c, int) else s
                    nc.vector.tensor_tensor(row(w_lo, c), raw_slots[slot], row(w_hi, c).bitcast(F32), ALU.subtract
                                            ).then_inc(w_lo_done, 1)

            def edge_list():
                steps = [0]

                def then_next(ins):
                    steps[0] += 1
                    ins.then_inc(prep, 1)
                    dve.wait_ge(prep, steps[0])

                dve.wait_ge(edges_in, 16 * 6)
                own = slice(WINDOW, WINDOW + EC)
                dst_hi, dst_lo, src_hi, src_lo = (p[0:EP, :] for p in e_part)
                nc.vector.scalar_tensor_tensor(key[0:EP, :], e_dst[0:EP, :], float(KEY_SHIFT), e_src[0:EP, :],
                                               ALU.mult, ALU.add)
                nc.vector.tensor_tensor(falls[0:EP, :], e_dst[0:EP, WINDOW + 1:WINDOW + 1 + EC], e_dst[0:EP, own], ALU.is_lt)
                then_next(nc.vector.tensor_tensor(long[0:EP, :], e_dst[0:EP, 2 * WINDOW:2 * WINDOW + EC], e_dst[0:EP, own], ALU.is_le))
                then_next(nc.vector.tensor_tensor(falls[0:EP, :], falls[0:EP, :], long[0:EP, :], ALU.add))
                nc.vector.tensor_tensor(loops[0:EP, :], e_dst[0:EP, own], e_src[0:EP, own], ALU.is_equal)
                then_next(nc.vector.tensor_reduce(bad[0:EP, 0:1], falls[0:EP, :], AX_X, ALU.add))
                nc.vector.memset(bad[0:EP, 2:3], 0.0).then_inc(bad_ready, 1)
                for ids, hi, lo in ((e_dst, dst_hi, dst_lo), (e_src, src_hi, src_lo)):
                    nc.vector.tensor_scalar(hi, ids[0:EP, own], 7, None, ALU.logical_shift_right)
                    then_next(nc.vector.tensor_scalar(lo, ids[0:EP, own], P - 1, None, ALU.bitwise_and))
                for index, r_hi, r_lo, s_hi, s_lo in ((idx_in, dst_hi, dst_lo, src_hi, src_lo),
                                                      (idx_out, src_hi, src_lo, dst_hi, dst_lo)):
                    at = index[0:EP, :]
                    then_next(nc.vector.scalar_tensor_tensor(at, s_hi, float(P), r_lo, ALU.mult, ALU.add))
                    then_next(nc.vector.scalar_tensor_tensor(at, s_lo, float(BLOCK), at, ALU.mult, ALU.add))
                    then_next(nc.vector.scalar_tensor_tensor(at, r_hi, float(P * BLOCK), at, ALU.mult, ALU.add))
                dve.wait_ge(bad_summed, 1)
                nc.vector.tensor_scalar(flag[0:1, 0:1], count[0:1, 0, 0:1], 0.0, None, ALU.is_gt).then_inc(flag_ready, 1)
                dve.wait_ge(flag_ready, 1)
                general = dve.value_load(flag[0:1, 0:1], min_val=0, max_val=1)
                found = outb[0:EP, 0, 0:EC]
                with dve.If(general > 0):
                    with dve.Fori(0, E // KEY_LOAD) as n:
                        with dve.Fori(0, KEY_LOAD // PAIR_KEYS) as m:
                            c = n * (KEY_LOAD // PAIR_KEYS) + m
                            eq = adj[0:EP, 1, :].rearrange("p (e k) -> p e k", k=PAIR_KEYS)
                            mine = key[0:EP, own].unsqueeze(2).broadcast_to([EP, EC, PAIR_KEYS])
                            all_of = bias[0:EP, bass.ds(m * PAIR_KEYS, PAIR_KEYS)].unsqueeze(1).broadcast_to([EP, EC, PAIR_KEYS])
                            dve.wait_ge(keys_in, (n + 1) * 16)
                            nc.vector.tensor_tensor(eq, mine, all_of, ALU.is_equal).then_inc(keys_used, 1)
                            dve.wait_ge(keys_used, c + 2)
                            nc.vector.tensor_reduce(found, eq.bitcast(F32), AX_X, ALU.add).then_inc(pair_eq, 1)
                            dve.wait_ge(pair_eq, c + 1)
                            nc.vector.tensor_tensor(pairs[0:EP, :], pairs[0:EP, :], found, ALU.add).then_inc(pair_sum, 1)
                            dve.wait_ge(pair_sum, c + 1)
                nc.vector.memset(bad[0:EP, 1:2], 0.0).then_inc(flag_ready, 1)

            def repeats(b):
                STEPS = 9
                cols = bass.ds(b * BATCH, BATCH)
                before, behind, times, skip = (repeat[0:EP, k, :] for k in range(4))
                eq = adj[0:EP, 1, 0:BATCH * WINDOW].rearrange("p (c w) -> p c w", w=WINDOW)
                own = key[0:EP, bass.ds(b * BATCH + WINDOW, BATCH)].unsqueeze(2).broadcast_to([EP, BATCH, WINDOW])
                for k, (first, found) in enumerate(((0, before), (WINDOW + 1, behind))):
                    near = windows(key[0:EP, bass.ds(b * BATCH + first, BATCH)])
                    nc.vector.tensor_tensor(eq, own, near, ALU.is_equal).then_inc(same, 1)
                    dve.wait_ge(same, b * STEPS + 2 * k + 1)
                    nc.vector.tensor_reduce(found, eq.bitcast(F32), AX_X, ALU.add).then_inc(same, 1)
                    dve.wait_ge(same, b * STEPS + 2 * k + 2)
                nc.vector.scalar_tensor_tensor(times, before, 1.0, behind, ALU.add, ALU.add).then_inc(same, 1)
                nc.vector.tensor_scalar(skip, before, 0.0, float(SKIP), ALU.is_gt, ALU.mult).then_inc(same, 1)
                dve.wait_ge(same, b * STEPS + 6)
                nc.vector.tensor_tensor(mult[0:EP, cols], times, pairs[0:EP, cols], ALU.max).then_inc(same, 1)
                nc.vector.tensor_tensor(idx_out[0:EP, cols], idx_out[0:EP, cols], skip, ALU.add).then_inc(same, 1)
                dve.wait_ge(same, b * STEPS + 8)
                nc.vector.tensor_tensor(loops[0:EP, cols], loops[0:EP, cols], mult[0:EP, cols], ALU.add).then_inc(same, 1)
                dve.wait_ge(same, b * STEPS + 9)
                nc.vector.tensor_tensor(idx_in[0:EP, cols], idx_in[0:EP, cols], skip, ALU.add).then_inc(batch_ready, 1)
                dve.wait_ge(batch_ready, b + 1)

            def windows(ap):
                return bass.AP(tensor=ap.tensor, offset=ap.offset, ap=[*ap.ap, [1, WINDOW]])

            def degrees(t, s):
                nc.vector.tensor_scalar(degc[:, s:s + 1], count[:, s, 0:1], 1.0, None, ALU.max).then_inc(deg_step, 1)
                dve.wait_ge(deg_step, 2 * t + 1)
                nc.vector.reciprocal(dinv[:, bass.ds(t, 1)], degc[:, s:s + 1]).then_inc(deg_step, 1)
                nc.vector.tensor_reduce(dpart[:, s, :], adj[:, s, :].bitcast(F32).rearrange("p (a r) -> p a r", r=P), AX_X, ALU.add
                                        ).then_inc(dsum_part, 1)
                dve.wait_ge(dsum_part, t + 1)
                nc.vector.tensor_tensor(dsum[:, :], dsum[:, :], dpart[:, s, :], ALU.add).then_inc(dsum_done, 1)
                dve.wait_ge(dsum_done, t + 1)
                dve.wait_ge(deg_step, 2 * t + 2)

            def norm(q, t, s):
                n = (0 if q == MEAN1 else NT) + t + 1
                for c in range(NC):
                    nc.vector.bn_stats(stats[:, s, c, :], outb[:, s, c * PSUM_COLS:(c + 1) * PSUM_COLS]).then_inc(stats_done, 1)
                dve.wait_ge(stats_done, n * NC)
                nc.vector.memset(scrap_dve[:, :], 0.0)
                nc.vector.bn_aggr(mv[:, s, :], stats[:, s, :, :]).then_inc(mv_done, 1)
                dve.wait_ge(mv_done, n)
                nc.vector.tensor_scalar(var[:, s:s + 1], mv[:, s, 1:2], EPS, None, ALU.add).then_inc(rstd_step, 1)
                dve.wait_ge(std_done, n)
                nc.vector.reciprocal(rstd[:, s:s + 1], std[:, s:s + 1]).then_inc(rstd_step, 1)
                newton(rstd[:, s:s + 1], var[:, s:s + 1], std[:, s:s + 1], rstd_step, n * 6 - 4)
                nc.vector.tensor_scalar(outb[:, s, :], outb[:, s, :], mv[:, s, 0:1], rstd[:, s:s + 1], ALU.subtract, ALU.mult
                                        ).then_inc(norm_done, 1)

            def newton(root, value, spare, step, done):
                dve.wait_ge(step, done)
                nc.vector.tensor_tensor(spare, root, root, ALU.mult).then_inc(step, 1)
                dve.wait_ge(step, done + 1)
                nc.vector.tensor_tensor(spare, spare, value, ALU.mult).then_inc(step, 1)
                dve.wait_ge(step, done + 2)
                nc.vector.tensor_scalar(spare, spare, -0.5, 1.5, ALU.mult, ALU.add).then_inc(step, 1)
                dve.wait_ge(step, done + 3)
                nc.vector.tensor_tensor(root, root, spare, ALU.mult).then_inc(step, 1)
                dve.wait_ge(step, done + 4)

            def evict(q, t, pair, s):
                z = outb[:, s, :]
                if q in (NEIGH0, NEIGH1):
                    dve.wait_ge(u_hi_done, (0 if q == NEIGH0 else NT) + t + 1)
                    nc.vector.tensor_tensor(row(u_lo, t), acc[:, s, :], row(u_hi, t).bitcast(F32), ALU.subtract).then_inc(acc_free, 1)
                    return
                dve.wait_ge(acc_full, q * NT + t + 1)
                if q in STORE:
                    dve.wait_ge(stored[s], 16 * (STORE[q] * PAIRS + pair + 1))
                elif q == GCN_LIN:
                    dve.wait_ge(stored[s], 16 * ((STORE[MEAN1] + 1) * PAIRS + 1))
                if q in biases:
                    dve.wait_ge(bias_full, 16 * (list(biases).index(q) + 1))
                    nc.vector.tensor_tensor(z, acc[:, s, :], bias[:, :], ALU.add).then_inc(acc_free, 1)
                if q == SELF1:
                    dve.wait_ge(acc_free, SLOTS + q * NT + t + 1)
                    dve.wait_ge(xin_full[s], 16 * (XIN[q] * PAIRS + pair + 1))
                    nc.vector.tensor_tensor(z, z, xin[:, s, :], ALU.add).then_inc(res_done, 1)
                elif q == GCN_LIN:
                    dve.wait_ge(u_hi_done, 2 * NT + t + 1)
                    nc.vector.scalar_tensor_tensor(row(u_lo, t), z, dscale[:, bass.ds(t, 1)], row(u_hi, t).bitcast(F32),
                                                   ALU.mult, ALU.subtract).then_inc(u_lo_done, 1)
                elif q in AGG:
                    if q == MEAN0:
                        degrees(t, s)
                    scale = dscale if q == GCN_AGG else dinv
                    dve.wait_ge(xin_full[s], 16 * (XIN[q] * PAIRS + pair + 1))
                    nc.vector.scalar_tensor_tensor(z, acc[:, s, :], scale[:, bass.ds(t, 1)], xin[:, s, :], ALU.mult, ALU.add
                                                   ).then_inc(acc_free, 1)
                    dve.wait_ge(acc_free, SLOTS + q * NT + t + 1)
                    if q == MEAN0:
                        nc.vector.tensor_scalar(z, z, 0.0, None, ALU.max).then_inc(relu_done, 1)
                    else:
                        norm(q, t, s)

            nc.vector.memset(eps[:, :], EPS).then_inc(eps_ready, 1)
            nc.vector.memset(ones[:, :].bitcast(F32), 1.0).then_inc(ones_ready, 1)
            nc.vector.memset(ones_f[:, :], 1.0).then_inc(ones_ready, 1)
            nc.vector.memset(ones_nt[:, :], 1.0).then_inc(ones_ready, 1)
            nc.vector.memset(dsum[:, :], 0.0).then_inc(dsum_zero, 1)
            nc.vector.memset(pairs[:, :], 0.0).then_inc(keys_used, 1)
            for s in range(SLOTS):
                nc.vector.memset(degc[:, s:s + 1], 0.0).then_inc(acc_free, 1)
                nc.vector.memset(std[:, s:s + 1], 0.0).then_inc(stored[s], 16)
                nc.vector.memset(rstd[:, s:s + 1], 0.0).then_inc(xt_stored[s], 16)
            dve.wait_ge(dsum_zero, 1)
            dve.wait_ge(keys_used, 1)
            turn_lo(0, 0, 0)
            for c in range(KD):
                split_lo(0, c, c)
            edge_list()
            for q in range(8):
                def body(t, pair, s, chunk, q=q):
                    last = isinstance(t, int) and t == NT - 1
                    if q in TURN and not last:
                        turn_lo(TURN[q], t + 1, 1 - s)
                    elif last and q + 1 in TURN:
                        turn_lo(TURN[q + 1], 0, 0)
                    elif last and q + 1 in LIN:
                        for c in range(KD):
                            split_lo(LIN[q + 1], c, c)
                    if q == NEIGH0:
                        repeats(t)
                    evict(q, t, pair, s)
                    if q in AGG and q + 1 in LIN and chunk is not None:
                        split_lo(LIN[q + 1], chunk, s)
                tiles(dve, body)
                if q == MEAN0:
                    nc.vector.tensor_scalar(dsum[:, :], dsum[:, :], 1.0, None, ALU.add).then_inc(dscale_step, 1)
                    dve.wait_ge(dsqrt_done, 1)
                    nc.vector.reciprocal(dscale[:, :], dsqrt[:, :]).then_inc(dscale_step, 1)
                    newton(dscale[:, :], dsum[:, :], dsqrt[:, :], dscale_step, 2)

        @block.tensor
        def _(pe):
            def turn_tile(q, t, pair, s):
                pe.wait_ge(xin_full[s], 16 * (XIN[q] * PAIRS + pair + 1))
                for k in range(KD):
                    ins = nc.tensor.transpose(turned[:, k * P:(k + 1) * P], xin[:, s, k * P:(k + 1) * P], ident[:, :])
                ins.then_inc(xt_turned, 1)

            def turn_weights(c, s):
                pe.wait_ge(raw_full[s], raw_wait(LIN[GCN_LIN], c, s))
                pe.wait_ge(w_lo_done, LIN[GCN_LIN] * KD + c)
                for k in range(KD):
                    ins = nc.tensor.transpose(turned[:, k * P:(k + 1) * P], raw[:, s, k * P:(k + 1) * P], ident[:, :])
                ins.then_inc(wt_turned, 1)

            def linear(q, t, pair, s):
                l = LIN[q]
                last = isinstance(t, int) and t == NT - 1
                if q in TURN:
                    pe.wait_ge(xt_lo_done, TURN[q] * NT + t + 1)
                else:
                    pe.wait_ge(xt_full[s], 32 * ((0 if q == SELF0 else PAIRS) + pair + 1))
                pe.wait_ge(acc_free, q * NT + t + 1)
                for k in range(KD):
                    if k == KD // 2 and q in TURN and not last:
                        turn_tile(q, t + 1, pair + s, 1 - s)
                    if s == 0:
                        pe.wait_ge(w_lo_done, l * KD + (k + 1 if l != LIN[GCN_LIN] else KD))
                    left = [part[:, s, k * P:(k + 1) * P] for part in (xt_hi, xt_lo)]
                    for a, right in ((left[0], w_hi), (left[0], w_lo), (left[1], w_hi)):
                        for n in range(NC):
                            cols = slice(n * PSUM_COLS, (n + 1) * PSUM_COLS)
                            ins = nc.tensor.matmul(acc[:, s, cols], a, right[:, k, cols], start=(k == 0 and right is w_hi and a is left[0]),
                                                   stop=(k == KD - 1 and a is left[1]))
                    if k == KD - 1:
                        ins.then_inc(acc_full, 1)
                    elif s == SLOTS - 1:
                        ins.then_inc(w_used, 1)

            def aggregate(q, t, pair, s, chunk, exact):
                def typed(ap):
                    return ap.bitcast(F32) if exact else ap
                pe.wait_ge(acc_free, q * NT + t + 1)
                pe.wait_ge(adj_full[s], 16 * (AGG[q] * PAIRS + pair + 1))
                for k in range(NT):
                    if k == NT // 2 and isinstance(t, int) and t == NT - 1 and q + 1 in LIN:
                        if q == MEAN1:
                            pe.wait_ge(w_lo_done, (LIN[GCN_LIN] + 1) * KD)
                        turn_tile(q + 1, 0, 0, 0)
                    if q == GCN_AGG and s == 0:
                        pe.wait_ge(u_lo_done, k + 1)
                    n_k = rows(k)
                    a = typed(adj[0:n_k, s, k * P:(k + 1) * P])
                    if q == MEAN0:
                        nc.tensor.matmul(count[:, s, 0:2], a, typed(ones[0:n_k, :]), start=(k == 0), stop=(k == NT - 1))
                    for part in (u_hi, u_lo):
                        for n in range(NC):
                            cols = slice(n * PSUM_COLS, (n + 1) * PSUM_COLS)
                            ins = nc.tensor.matmul(acc[:, s, cols], a, typed(part[0:n_k, k, cols]),
                                                   start=(k == 0 and part is u_hi), stop=(k == NT - 1 and part is u_lo))
                ins.then_inc(acc_full, 1)
                if q == MEAN1 and chunk is not None:
                    turn_weights(chunk, s)

            pe.wait_ge(ident_ready, 1)
            pe.wait_ge(ones_ready, 2)
            turn_tile(NEIGH0, 0, 0, 0)
            pe.wait_ge(bad_ready, 1)
            nc.tensor.matmul(count[0:1, 0, 0:1], bad[0:EP, 0:1], ones_f[0:EP, :], start=True, stop=True).then_inc(bad_summed, 1)
            for q in range(8):
                if q in LIN:
                    tiles(pe, lambda t, pair, s, chunk, q=q: linear(q, t, pair, s))
                    continue
                if q == MEAN0:
                    pe.wait_ge(flag_ready, 2)
                    general = pe.value_load(flag[0:1, 0:1], min_val=0, max_val=1)
                with pe.If(general > 0):
                    tiles(pe, lambda t, pair, s, chunk, q=q: aggregate(q, t, pair, s, chunk, True))
                with pe.Else():
                    tiles(pe, lambda t, pair, s, chunk, q=q: aggregate(q, t, pair, s, chunk, False))


_INS = ["x", "src", "dst", "L0_gnn_W_self0", "L0_gnn_W_neigh0", "L0_gnn_b0", "L0_gnn_W_self1", "L0_gnn_W_neigh1", "L0_gnn_b1",
        "L1_gnn_W", "L1_gnn_b"]


def kernel(**inputs):
    import numpy as _np
    import concourse.bacc as _bacc
    from concourse import mybir as _mybir
    from concourse.bass_utils import run_bass_kernel_spmd as _run

    nc = _bacc.Bacc("TRN2", target_bir_lowering=False, num_devices=1)
    arrays, args = {}, []
    for name in _INS:
        a = _np.ascontiguousarray(inputs[name])
        arrays[f"in_{name}"] = a
        args.append(nc.dram_tensor(f"in_{name}", a.shape, _mybir.dt.from_np(a.dtype), kind="ExternalInput").ap())
    shape = inputs["x"].shape
    args.append(nc.dram_tensor("out", shape, _mybir.dt.float32, kind="ExternalOutput").ap())
    build(nc, *args)
    r = _run(nc, [arrays], core_ids=[0])
    return r.results[0]["out"]
```

```python
from contextlib import ExitStack

import concourse.bass as bass
from concourse import mybir

P = 128
PSUM_COLS = 512
WINDOW = 48
NO_NODE = 4095
SKIP = 1 << 22
KEY_SHIFT = 2048
EPS = 1e-5

F32 = mybir.dt.float32
F32R = mybir.dt.float32r
I32 = mybir.dt.int32
ACT = mybir.ActivationFunctionType
ALU = mybir.AluOpType
AX_X = mybir.AxisListType.X


def build(nc, x, src, dst, w_self0, w_neigh0, b0, w_self1, w_neigh1, b1, w_gcn, b_gcn, out):
    N, D = x.shape
    E = src.shape[0]
    NT = -(-N // P)
    LAST = N - (NT - 1) * P
    KD = D // P
    NC = D // PSUM_COLS
    EP = 125
    EC = E // EP
    BATCH = EC // NT
    SLOTS = 2
    CELL_STEPS = 12
    LAG = 2
    PAIRS = NT // SLOTS
    BLOCK = NT * P
    CELLS = NT * P * BLOCK
    HALO = EC + 2 * WINDOW
    PAIR_KEYS = BLOCK // EC
    ZEROS = 2 * P
    KEY_LOAD = 1000
    assert E == EP * EC and EC % NT == 0 and NT % SLOTS == 0 and KD % SLOTS == 0
    assert E % KEY_LOAD == 0 and KEY_LOAD % PAIR_KEYS == 0 and KEY_LOAD <= D
    assert BATCH * WINDOW <= BLOCK and N < KEY_SHIFT - 1 and SKIP > CELLS

    NEIGH0, SELF0, MEAN0, NEIGH1, SELF1, MEAN1, GCN_LIN, GCN_AGG = range(8)
    LIN = {NEIGH0: 0, SELF0: 1, NEIGH1: 2, SELF1: 3, GCN_LIN: 4}
    AGG = {MEAN0: 0, MEAN1: 1, GCN_AGG: 2}
    TURN = {NEIGH0: 0, NEIGH1: 1, GCN_LIN: 2}
    XIN = {NEIGH0: 0, MEAN0: 1, NEIGH1: 2, SELF1: 3, MEAN1: 4, GCN_LIN: 5, GCN_AGG: 6}
    STORE = {SELF0: 0, MEAN0: 1, SELF1: 2, MEAN1: 3, GCN_AGG: 4}

    with ExitStack() as ctx:
        def sb(name, shape, dt):
            return ctx.enter_context(nc.sbuf_tensor(name, shape, dt))

        def sem(name):
            return ctx.enter_context(nc.semaphore(name))

        def dram(name, shape, dt=F32):
            return nc.dram_tensor(name, shape, dt, kind="Internal").ap()

        self_scr = dram("self_scr", [NT * P, D])
        h_scr = dram("h_scr", [NT * P, D])
        y_scr = dram("y_scr", [NT * P, D])
        xt_hi_scr = dram("xt_hi_scr", [NT * P, D])
        xt_lo_scr = dram("xt_lo_scr", [NT * P, D])
        wt_scr = dram("wt_scr", [D, D])
        keys_scr = dram("keys_scr", [E])
        adj_in = dram("adj_in", [CELLS, 1])
        adj_out = dram("adj_out", [CELLS, 1])

        u_hi = sb("u_hi", [P, NT, D], F32R)
        u_lo = sb("u_lo", [P, NT, D], F32R)
        w_hi = sb("w_hi", [P, KD, D], F32R)
        w_lo = sb("w_lo", [P, KD, D], F32R)
        xt_hi = sb("xt_hi", [P, SLOTS, D], F32R)
        xt_lo = sb("xt_lo", [P, SLOTS, D], F32R)
        adj = sb("adj", [P, SLOTS, BLOCK], F32R)

        xin = sb("xin", [P, SLOTS, D], F32)
        raw = sb("raw", [P, SLOTS, D], F32)
        outb = sb("outb", [P, SLOTS, D], F32)
        bias = sb("bias", [P, D], F32)
        zeros = sb("zeros", [P, ZEROS], F32)
        ident = sb("ident", [P, P], F32)
        key = sb("key", [P, HALO], F32)
        idx_in = sb("idx_in", [P, EC], I32)
        idx_out = sb("idx_out", [P, EC], I32)
        mult = sb("mult", [P, EC], F32)
        loops = sb("loops", [P, EC], F32)
        ones_nt = sb("ones_nt", [P, NT], F32)
        pairs = sb("pairs", [P, EC], F32)
        repeat = sb("repeat", [P, 4, BATCH], F32)
        idx_slot = sb("idx_slot", [P, SLOTS, BATCH], I32)
        mult_slot = sb("mult_slot", [P, SLOTS, BATCH], F32)
        bad = sb("bad", [P, 4], F32)
        flag = sb("flag", [P, 2], I32)
        dinv = sb("dinv", [P, NT], F32)
        degc = sb("degc", [P, SLOTS], F32)
        dsum = sb("dsum", [P, NT], F32)
        dpart = sb("dpart", [P, SLOTS, NT], F32)
        dsqrt = sb("dsqrt", [P, NT], F32)
        dscale = sb("dscale", [P, NT], F32)
        stats = sb("stats", [P, SLOTS, NC, 6], F32)
        mv = sb("mv", [P, SLOTS, 2], F32)
        std = sb("std", [P, SLOTS], F32)
        var = sb("var", [P, SLOTS], F32)
        rstd = sb("rstd", [P, SLOTS], F32)
        eps = sb("eps", [P, 1], F32)
        scrap_dve = sb("scrap_dve", [P, 1], F32)
        scrap_act = sb("scrap_act", [P, 1], F32)
        scrap_pool = sb("scrap_pool", [P, 1 + BATCH], F32)
        ones = sb("ones", [P, 1], F32)
        in_part = sb("in_part", [P, SLOTS, P], F32)

        e_dst = bias[:, 0:HALO].bitcast(I32)
        e_src = bias[:, HALO:2 * HALO].bitcast(I32)
        e_part = [*(bias[:, 2 * HALO + i * EC:2 * HALO + (i + 1) * EC].bitcast(I32) for i in range(3)), mult[:, :].bitcast(I32)]
        falls, long = (idx[:, :].bitcast(F32) for idx in (idx_in, idx_out))
        assert 2 * HALO + 3 * EC <= D

        raw_slots = [raw[:, 0, :], raw[:, 1, :], outb[:, 0, :], outb[:, 1, :]]

        acc = ctx.enter_context(nc.psum_tensor("acc", [P, SLOTS, D], F32))
        turned = ctx.enter_context(nc.psum_tensor("turned", [P, D], F32))
        count = ctx.enter_context(nc.psum_tensor("count", [P, SLOTS, PSUM_COLS], F32))

        edges_in = sem("edges_in")
        halo_set = sem("halo_set")
        ident_zero = sem("ident_zero")
        ident_ready = sem("ident_ready")
        ones_ready = sem("ones_ready")
        zeros_ready = sem("zeros_ready")
        cleared_in = sem("cleared_in")
        cleared_out = sem("cleared_out")
        diagonal_set = sem("diagonal_set")
        prep = sem("prep")
        parts_ready = sem("parts_ready")
        cell_step = sem("cell_step")
        bad_ready = sem("bad_ready")
        bad_summed = sem("bad_summed")
        flag_ready = sem("flag_ready")
        keys_out = sem("keys_out")
        keys_in = sem("keys_in")
        keys_used = sem("keys_used")
        pair_eq = sem("pair_eq")
        pair_sum = sem("pair_sum")
        same = sem("same")
        batch_ready = sem("batch_ready")
        batch_copied = sem("batch_copied")
        scattered = [sem(f"scattered{s}") for s in range(SLOTS)]
        wt_turned = sem("wt_turned")
        wt_copied = sem("wt_copied")
        wt_stored = [sem(f"wt_stored{s}") for s in range(SLOTS)]
        xin_full = [sem(f"xin_full{s}") for s in range(SLOTS)]
        raw_full = [sem(f"raw_full{s}") for s in range(2 * SLOTS)]
        xt_stored = [sem(f"xt_stored{s}") for s in range(SLOTS)]
        xt_full = [sem(f"xt_full{s}") for s in range(SLOTS)]
        adj_full = [sem(f"adj_full{s}") for s in range(SLOTS)]
        stored = [sem(f"stored{s}") for s in range(SLOTS)]
        bias_full = sem("bias_full")
        xt_turned = sem("xt_turned")
        xt_hi_done = sem("xt_hi_done")
        xt_lo_done = sem("xt_lo_done")
        w_hi_done = sem("w_hi_done")
        w_lo_done = sem("w_lo_done")
        w_used = sem("w_used")
        acc_full = sem("acc_full")
        block_done = sem("block_done")
        block_full = sem("block_full")
        acc_free = sem("acc_free")
        u_hi_done = sem("u_hi_done")
        u_lo_done = sem("u_lo_done")
        res_done = sem("res_done")
        deg_step = sem("deg_step")
        dsum_zero = sem("dsum_zero")
        in_part_done = sem("in_part_done")
        dsum_part = sem("dsum_part")
        dsum_done = sem("dsum_done")
        dsqrt_done = sem("dsqrt_done")
        dscale_step = sem("dscale_step")
        relu_done = sem("relu_done")
        stats_done = sem("stats_done")
        mv_done = sem("mv_done")
        std_done = sem("std_done")
        rstd_step = sem("rstd_step")
        norm_done = sem("norm_done")
        eps_ready = sem("eps_ready")

        sources = {NEIGH0: x, MEAN0: self_scr, NEIGH1: h_scr, SELF1: x, MEAN1: self_scr, GCN_LIN: y_scr, GCN_AGG: y_scr}
        made_by = {MEAN0: SELF0, NEIGH1: MEAN0, MEAN1: SELF1, GCN_LIN: MEAN1, GCN_AGG: MEAN1}
        results = {SELF0: self_scr, MEAN0: h_scr, SELF1: self_scr, MEAN1: y_scr, GCN_AGG: out}
        weights = [w_neigh0, w_self0, w_neigh1, w_self1, wt_scr]
        biases = {SELF0: b0, SELF1: b1, GCN_LIN: b_gcn}

        def is_end(q, t):
            return q == GCN_AGG and isinstance(t, int) and t == NT - 1

        def rows(t):
            return LAST if isinstance(t, int) and t == NT - 1 else P

        def tiles(eng, body):
            with eng.Fori(0, PAIRS - 1) as i:
                for s in range(SLOTS):
                    body(i * SLOTS + s, i, s, i * SLOTS + s)
            for s in range(SLOTS):
                body(NT - SLOTS + s, PAIRS - 1, s, None)

        def raw_slot(l, c):
            return c % (2 * SLOTS) if l in (LIN[NEIGH0], LIN[SELF0], LIN[SELF1]) else c % SLOTS

        def raw_count(l, c):
            turned_before = KD // SLOTS if l > LIN[SELF0] and raw_slot(l, c) < SLOTS else 0
            before = turned_before + sum(raw_slot(m, d) == raw_slot(l, c) for m in range(l) for d in range(KD))
            return before + sum(raw_slot(l, d) == raw_slot(l, c) for d in range(c + 1))

        def raw_wait(l, c, s):
            if isinstance(c, int):
                return 16 * raw_count(l, c)
            return 16 * raw_count(l, s) + 8 * (c - s)

        def row(buf, t):
            return buf[:, bass.ds(t, 1), :].rearrange("p a d -> p (a d)")

        def gcn_wait(pair, s):
            return 16 * (raw_count(LIN[SELF0], 2 * SLOTS + s) + 1) + 16 * pair

        block = ctx.enter_context(nc.Block())

        @block.sync
        def _(sp):
            def load_weights(l, c, s):
                if not isinstance(c, int):
                    sp.wait_ge(w_lo_done, l * KD + c - SLOTS + 1)
                elif l == LIN[NEIGH1] and c < SLOTS:
                    sp.wait_ge(wt_stored[s], 16 * KD // SLOTS)
                elif l == LIN[SELF1] and SLOTS <= c < 2 * SLOTS:
                    sp.wait_ge(stored[s % SLOTS], 16 * ((STORE[MEAN0] + 1) * PAIRS + 1))
                elif l > 0 or c >= 2 * SLOTS:
                    chunks = [m * KD + d for m in range(l + 1) for d in range(KD)
                              if m * KD + d < l * KD + c and raw_slot(m, d) == raw_slot(l, c)]
                    sp.wait_ge(w_lo_done, chunks[-1] + 1)
                slot = s if not isinstance(c, int) else raw_slot(l, c)
                sp.dma_start(raw_slots[slot], weights[l][bass.ds(c * P, P), :]).then_inc(raw_full[slot], 16)

            def load_gcn(c, pair, s):
                if isinstance(c, int):
                    sp.wait_ge(w_lo_done, LIN[SELF0] * KD + 2 * SLOTS + c + 1)
                else:
                    sp.wait_ge(wt_stored[s], 16 * pair)
                sp.dma_start(raw[:, s, :], w_gcn[bass.ds(c * P, P), :]).then_inc(raw_full[s], 16)

            def load_tile(q, t, pair, s):
                before, t_before = q, t - SLOTS
                if isinstance(t, int) and t < SLOTS:
                    before = next((p for p in XIN if XIN[p] == XIN[q] - 1), None)
                    t_before = NT - SLOTS + s
                if before in TURN:
                    sp.wait_ge(xt_turned, TURN[before] * NT + t_before + 1)
                elif before == SELF1:
                    sp.wait_ge(res_done, t_before + 1)
                elif before in AGG:
                    sp.wait_ge(acc_free, SLOTS + before * NT + t_before + 1)
                if q in made_by:
                    sp.wait_ge(stored[s], 16 * (STORE[made_by[q]] * PAIRS + pair + 2))
                n = rows(t) if sources[q] is x else P
                sp.dma_start(xin[0:n, s, :], sources[q][bass.ds(t * P, n), :]).then_inc(xin_full[s], 16)

            def load_turned(q, t, s):
                sp.wait_ge(acc_full, q * NT + t - SLOTS + 1)
                if isinstance(t, int) and t < SLOTS:
                    sp.wait_ge(xt_stored[s], 16 + 32 * (TURN[q - 1] + 1) * PAIRS)
                for scr, buf in ((xt_hi_scr, xt_hi), (xt_lo_scr, xt_lo)):
                    sp.dma_start(buf[:, s, :].bitcast(F32), scr[bass.ds(t * P, P), :]).then_inc(xt_full[s], 16)

            def load_adj(q, t, s):
                first = isinstance(t, int) and t < SLOTS
                if q == MEAN1 and first:
                    sp.wait_ge(dsum_part, NT - SLOTS + s + 1)
                elif q == GCN_AGG and first:
                    sp.wait_ge(acc_full, MEAN1 * NT + NT - SLOTS + s + 1)
                elif q == MEAN0 and not first:
                    sp.wait_ge(dsum_part, t - SLOTS + 1)
                elif not first:
                    sp.wait_ge(acc_full, q * NT + t - SLOTS + 1)
                table = (adj_out if q == GCN_AGG else adj_in).rearrange("(a p b) o -> a p (b o)", p=P, b=BLOCK)
                sp.dma_start(adj[:, s, :].bitcast(F32), table[bass.ds(t, 1), :, :].rearrange("a p b -> (a p) b")
                             ).then_inc(adj_full[s], 16)

            def load_bias(q):
                if q == SELF0:
                    sp.wait_ge(batch_ready, 1)
                else:
                    sp.wait_ge(acc_free, SLOTS + ({SELF1: SELF0, GCN_LIN: SELF1}[q] + 1) * NT)
                sp.dma_start(bias[:, :], biases[q].rearrange("(a d) -> a d", a=1).broadcast_to([P, D])).then_inc(bias_full, 16)

            def tile(q, t, pair, s):
                if q in AGG:
                    load_adj(q, t, s)
                if q in (SELF0, SELF1):
                    load_turned(q, t, s)
                if q in XIN:
                    load_tile(q, t, pair, s)
                if q == SELF0 and not isinstance(t, int):
                    load_gcn(t, pair, s)
                if q in AGG:
                    if q + 1 in LIN and not (isinstance(t, int) and t >= KD):
                        load_weights(LIN[q + 1], t, s)

            def other_tiles(q):
                with sp.Fori(1, PAIRS - 1) as i:
                    for s in range(SLOTS):
                        tile(q, i * SLOTS + s, i, s)
                for s in range(SLOTS):
                    tile(q, NT - SLOTS + s, PAIRS - 1, s)

            load_tile(NEIGH0, 0, 0, 0)
            sp.wait_ge(halo_set, 2)
            for ids, where in ((dst, e_dst), (src, e_src)):
                grid = ids.rearrange("(p c) -> p c", c=EC)
                sp.dma_start(where[0:EP, WINDOW:WINDOW + EC], grid).then_inc(edges_in, 16)
                sp.dma_start(where[1:EP, 0:WINDOW], grid[0:EP - 1, EC - WINDOW:EC]).then_inc(edges_in, 16)
                sp.dma_start(where[0:EP - 1, WINDOW + EC:HALO], grid[1:EP, 0:WINDOW]).then_inc(edges_in, 16)
            for c in range(KD):
                load_weights(LIN[NEIGH0], c, c)
            load_tile(NEIGH0, 1, 0, 1)
            other_tiles(NEIGH0)
            for q in range(1, 8):
                if q == SELF0:
                    load_bias(q)
                if q in LIN and q - 1 in LIN:
                    for c in range(2 * SLOTS):
                        load_weights(LIN[q], c, c)
                    tile(q, 0, 0, 0)
                    for c in range(2 * SLOTS, KD):
                        load_weights(LIN[q], c, c)
                    if q == SELF0:
                        load_gcn(0, 0, 0)
                    tile(q, 1, 0, 1)
                    if q == SELF0:
                        load_gcn(1, 0, 1)
                else:
                    if q == MEAN0:
                        for s in range(SLOTS):
                            sp.wait_ge(scattered[s], 16 * EC // SLOTS)
                    if q == GCN_AGG:
                        for s in range(SLOTS):
                            sp.wait_ge(scattered[s], 16 * EC)
                    for s in range(SLOTS):
                        tile(q, s, 0, s)
                if q in biases and q != SELF0:
                    load_bias(q)
                other_tiles(q)
            for s in range(SLOTS):
                sp.wait_ge(stored[s], 16 * ((STORE[GCN_AGG] + 1) * PAIRS + 1 + (NC - 1 if s == SLOTS - 1 else 0)))

        @block.gpsimd
        def _(pool):
            nc.gpsimd.memset(e_dst[0:EP, :], NO_NODE).then_inc(halo_set, 1)
            nc.gpsimd.memset(e_src[0:EP, :], NO_NODE).then_inc(halo_set, 1)
            nc.gpsimd.memset(ident[:, :], 0.0).then_inc(ident_zero, 1)
            pool.wait_ge(ident_zero, 1)
            nc.gpsimd.affine_select(out=ident[:, :], in_=ident[:, :], compare_op=ALU.not_equal, fill=1.0, base=0,
                                    pattern=[[-1, P]], channel_multiplier=1).then_inc(ident_ready, 1)
            nc.gpsimd.memset(zeros[:, :], 0.0).then_inc(zeros_ready, 1)
            pool.wait_ge(zeros_ready, 1)

            steps = [0]

            def then_next(ins):
                steps[0] += 1
                ins.then_inc(cell_step, 1)
                pool.wait_ge(cell_step, steps[0])

            def edge_cells():
                pool.wait_ge(parts_ready, 2)
                dst_hi, dst_lo, src_hi, src_lo = (p[0:EP, :] for p in e_part)
                for index, r_hi, r_lo, s_hi, s_lo in ((idx_in, dst_hi, dst_lo, src_hi, src_lo),
                                                      (idx_out, src_hi, src_lo, dst_hi, dst_lo)):
                    at = index[0:EP, :]
                    then_next(nc.gpsimd.tensor_scalar(at, r_hi, float(P), None, ALU.mult))
                    then_next(nc.gpsimd.tensor_tensor(at, at, s_lo, ALU.add))
                    then_next(nc.gpsimd.tensor_scalar(at, at, float(NT), None, ALU.mult))
                    then_next(nc.gpsimd.tensor_tensor(at, at, s_hi, ALU.add))
                    then_next(nc.gpsimd.tensor_scalar(at, at, float(P), None, ALU.mult))
                    then_next(nc.gpsimd.tensor_tensor(at, at, r_lo, ALU.add))

            def clear(table, a, done):
                block = table.rearrange("(a p b) o -> a p (b o)", p=P, b=BLOCK)[bass.ds(a, 1), :, :]
                pool.dma_start(block.rearrange("a p (c z) -> (a p) c z", z=ZEROS),
                               zeros[:, :].unsqueeze(1).broadcast_to([P, BLOCK // ZEROS, ZEROS])).then_inc(done, 16)

            def scatter(table, cleared, index, counts, scattered_before, in_turn):
                def batch(i, s):
                    b = i * SLOTS + s
                    pool.wait_ge(batch_ready, b + 1)
                    if scattered_before or not isinstance(i, int):
                        pool.wait_ge(scattered[s], (i + scattered_before * PAIRS) * (16 * BATCH))
                    cols = bass.ds(b * BATCH, BATCH)
                    nc.gpsimd.tensor_copy(idx_slot[0:EP, s, :], index[0:EP, cols]).then_inc(batch_copied, 1)
                    nc.gpsimd.tensor_copy(mult_slot[0:EP, s, :], counts[0:EP, cols]).then_inc(batch_copied, 1)
                    pool.wait_ge(cleared, 16 * NT)
                    pool.wait_ge(batch_copied, (b + 1 + scattered_before * NT) * 2)
                    nc.gpsimd.tensor_tensor(scrap_pool[0:EP, 0:1], mult_slot[0:EP, s, 0:1], mult_slot[0:EP, s, 0:1], ALU.add)
                    for j in range(BATCH):
                        pool.indirect_dma_start(
                            table, bass.IndirectOffsetOnAxis(ap=idx_slot[0:EP, s, j:j + 1], axis=0),
                            mult_slot[0:EP, s, j:j + 1], None, bounds_check=CELLS - 1, oob_is_err=False,
                        ).then_inc(scattered[s], 16)
                        if in_turn:
                            pool.wait_ge(scattered[s], (i + scattered_before * PAIRS) * (16 * BATCH) + 16 * (j + 1))
                            nc.gpsimd.tensor_tensor(scrap_pool[0:EP, j + 1:j + 2], mult_slot[0:EP, s, 0:1], mult_slot[0:EP, s, 0:1], ALU.add)
                    if not scattered_before:
                        clear(adj_out, b, cleared_out)

                for s in range(SLOTS):
                    batch(0, s)
                with pool.Fori(1, PAIRS) as i:
                    for s in range(SLOTS):
                        batch(i, s)

            edge_cells()
            pool.wait_ge(ones_ready, 2)
            pool.wait_ge(raw_full[raw_slot(0, KD - 1)], raw_wait(0, KD - 1, 0))
            for a in range(NT):
                clear(adj_in, a, cleared_in)
            pool.wait_ge(flag_ready, 1)
            general = pool.value_load(flag[0:1, 0:1], min_val=0, max_val=1)
            with pool.If(general > 0):
                pool.dma_start(keys_scr.rearrange("(p c) -> p c", c=EC), key[0:EP, WINDOW:WINDOW + EC]).then_inc(keys_out, 16)
                pool.wait_ge(keys_out, 16)
                spread = keys_scr.rearrange("(n k) -> n k", k=KEY_LOAD)
                with pool.Fori(0, E // KEY_LOAD) as n:
                    pool.wait_ge(keys_used, n * (KEY_LOAD // PAIR_KEYS) + 1)
                    pool.dma_start(bias[0:EP, 0:KEY_LOAD], spread[bass.ds(n, 1), :].broadcast_to([EP, KEY_LOAD])
                                   ).then_inc(keys_in, 16)
            with pool.If(general > 0):
                scatter(adj_in, cleared_in, idx_in, mult, 0, True)
            with pool.Else():
                scatter(adj_in, cleared_in, idx_in, mult, 0, False)
            pool.wait_ge(cleared_out, 16 * NT)
            diagonal = bass.AP(tensor=adj_out.tensor, offset=0, ap=[[BLOCK + 1, P], [P * BLOCK + P, NT]])
            pool.dma_start(diagonal, ones_nt[:, :], allow_slow_non_contiguous=True).then_inc(diagonal_set, 16)
            pool.wait_ge(diagonal_set, 16)
            with pool.If(general > 0):
                scatter(adj_out, cleared_out, idx_out, loops, 1, True)
            with pool.Else():
                scatter(adj_out, cleared_out, idx_out, loops, 1, False)

        @block.scalar
        def _(act):
            def turn_hi(n, t, s):
                act.wait_ge(xt_turned, n * NT + t + 1)
                if n < TURN[GCN_LIN]:
                    act.wait_ge(xt_stored[s], 16 + 32 * n * PAIRS + 16 * (t - s))
                else:
                    act.wait_ge(xt_stored[s], 16 + 32 * TURN[GCN_LIN] * PAIRS)
                nc.scalar.activation(xt_hi[:, s, :], turned[:, :], ACT.Copy).then_inc(xt_hi_done, 1)

            def split_hi(l, c, s):
                slot = raw_slot(l, c) if isinstance(c, int) else s
                act.wait_ge(raw_full[slot], raw_wait(l, c, s))
                if l in (LIN[NEIGH1], LIN[GCN_LIN]):
                    act.wait_ge(acc_full, ({LIN[NEIGH1]: SELF0, LIN[GCN_LIN]: SELF1}[l] + 1) * NT)
                elif l > 0 and c < KD - 1:
                    act.wait_ge(w_used, (l * PAIRS - 1) * (KD - 1) + c + 1)
                elif l > 0:
                    act.wait_ge(acc_full, {LIN[SELF0]: SELF0, LIN[SELF1]: SELF1}[l] * NT)
                nc.scalar.activation(row(w_hi, c), raw_slots[slot], ACT.Copy).then_inc(w_hi_done, 1)

            def store_gcn(c, s):
                act.wait_ge(wt_turned, c + 1)
                nc.scalar.activation(raw[:, s, :], turned[:, :], ACT.Copy).then_inc(wt_copied, 1)
                act.wait_ge(wt_copied, c + 2)
                act.dma_start(wt_scr.rearrange("(k p) o -> p k o", p=P)[:, :, bass.ds(c * P, P)],
                              raw[:, s, :].rearrange("p (k o) -> p k o", k=KD)).then_inc(wt_stored[s], 16)

            def store_turned(n, t, s):
                act.wait_ge(xt_lo_done, n * NT + t + 1)
                for scr, buf in ((xt_hi_scr, xt_hi), (xt_lo_scr, xt_lo)):
                    act.dma_start(scr[bass.ds(t * P, P), :], buf[:, s, :].bitcast(F32)).then_inc(xt_stored[s], 16)

            def store(q, t, s):
                if q == SELF0:
                    act.wait_ge(acc_free, SLOTS + q * NT + t + 1)
                elif q == SELF1:
                    act.wait_ge(res_done, t + 1)
                elif q == MEAN0:
                    act.wait_ge(relu_done, t + 1)
                elif is_end(q, t):
                    for c in range(NC):
                        cols = slice(c * PSUM_COLS, (c + 1) * PSUM_COLS)
                        act.wait_ge(norm_done, 2 * NT + c)
                        act.dma_start(out[t * P:N, cols], outb[0:LAST, s, cols]).then_inc(stored[s], 16)
                    return
                else:
                    act.wait_ge(norm_done, (0 if q == MEAN1 else NT) + t + 1)
                n = rows(t) if q == GCN_AGG else P
                act.dma_start(results[q][bass.ds(t * P, n), :], outb[0:n, s, :]).then_inc(stored[s], 16)

            def evict(q, t, s):
                if q in (NEIGH0, NEIGH1):
                    act.wait_ge(acc_full, q * NT + t + 1)
                    nc.scalar.activation(row(u_hi, t), acc[:, s, :], ACT.Copy).then_inc(u_hi_done, 1)
                elif q == GCN_LIN:
                    act.wait_ge(acc_free, SLOTS + q * NT + t + 1)
                    nc.scalar.activation(row(u_hi, t), outb[:, s, :], ACT.Copy, scale=dscale[:, bass.ds(t, 1)]
                                         ).then_inc(u_hi_done, 1)
                else:
                    if q in (MEAN1, GCN_AGG):
                        act.wait_ge(mv_done, (0 if q == MEAN1 else NT) + t + 1)
                        nc.scalar.activation(std[:, s:s + 1], mv[:, s, 1:2], ACT.Sqrt, bias=eps[:, 0:1]).then_inc(std_done, 1)
                    store(q, t, s)

            act.wait_ge(eps_ready, 1)
            nc.scalar.activation(scrap_act[:, :], eps[:, :], ACT.Copy)
            turn_hi(TURN[NEIGH0], 0, 0)
            for c in range(KD):
                split_hi(LIN[NEIGH0], c, c)
            store_turned(TURN[NEIGH0], 0, 0)
            for q in range(8):
                def body(t, pair, s, chunk, q=q):
                    last = isinstance(t, int) and t == NT - 1
                    if q in TURN and not last:
                        turn_hi(TURN[q], t + 1, 1 - s)
                    elif last and q + 1 in TURN:
                        turn_hi(TURN[q + 1], 0, 0)
                    elif last and q + 1 in LIN:
                        for c in range(KD):
                            if c == KD // 2:
                                evict(q, t, s)
                            split_hi(LIN[q + 1], c, c)
                        return
                    evict(q, t, s)
                    if q in (NEIGH0, NEIGH1) and not last:
                        store_turned(TURN[q], t + 1, 1 - s)
                    elif last and q + 1 == NEIGH1:
                        store_turned(TURN[q + 1], 0, 0)
                    if q == SELF0 and chunk is not None:
                        store_gcn(chunk, s)
                    if q in AGG and q + 1 in LIN and chunk is not None:
                        split_hi(LIN[q + 1], chunk, s)
                tiles(act, body)
                if q == MEAN0:
                    act.wait_ge(dscale_step, 1)
                    nc.scalar.activation(dsqrt[:, :], dsum[:, :], ACT.Sqrt).then_inc(dsqrt_done, 1)

        @block.vector
        def _(dve):
            def turn_lo(n, t, s):
                dve.wait_ge(xt_hi_done, n * NT + t + 1)
                nc.vector.tensor_tensor(xt_lo[:, s, :], turned[:, :], xt_hi[:, s, :].bitcast(F32), ALU.subtract
                                        ).then_inc(xt_lo_done, 1)

            def split_lo(l, c, s):
                dve.wait_ge(w_hi_done, l * KD + c + 1)
                slot = raw_slot(l, c) if isinstance(c, int) else s
                nc.vector.tensor_tensor(row(w_lo, c), raw_slots[slot], row(w_hi, c).bitcast(F32), ALU.subtract
                                        ).then_inc(w_lo_done, 1)

            steps = [0]
            own = slice(WINDOW, WINDOW + EC)

            def then_next(ins):
                steps[0] += 1
                ins.then_inc(prep, 1)
                dve.wait_ge(prep, steps[0])

            def edge_keys():
                dve.wait_ge(edges_in, 16 * 6)
                nc.vector.scalar_tensor_tensor(key[0:EP, :], e_dst[0:EP, :], float(KEY_SHIFT), e_src[0:EP, :],
                                               ALU.mult, ALU.add)
                nc.vector.tensor_tensor(falls[0:EP, :], e_dst[0:EP, WINDOW + 1:WINDOW + 1 + EC], e_dst[0:EP, own], ALU.is_lt)
                then_next(nc.vector.tensor_tensor(long[0:EP, :], e_dst[0:EP, 2 * WINDOW:2 * WINDOW + EC], e_dst[0:EP, own], ALU.is_le))
                then_next(nc.vector.tensor_tensor(falls[0:EP, :], falls[0:EP, :], long[0:EP, :], ALU.add))
                nc.vector.tensor_tensor(loops[0:EP, :], e_dst[0:EP, own], e_src[0:EP, own], ALU.is_equal)
                then_next(nc.vector.tensor_reduce(bad[0:EP, 0:1], falls[0:EP, :], AX_X, ALU.add))
                nc.vector.memset(bad[0:EP, 2:3], 0.0).then_inc(bad_ready, 1)

            def edge_parts():
                dst_hi, dst_lo, src_hi, src_lo = (p[0:EP, :] for p in e_part)
                for ids, hi, lo in ((e_dst, dst_hi, dst_lo), (e_src, src_hi, src_lo)):
                    nc.vector.tensor_scalar(hi, ids[0:EP, own], 7, None, ALU.logical_shift_right)
                    nc.vector.tensor_scalar(lo, ids[0:EP, own], P - 1, None, ALU.bitwise_and).then_inc(parts_ready, 1)

            def edge_form():
                dve.wait_ge(bad_summed, 1)
                nc.vector.tensor_scalar(flag[0:1, 0:1], count[0:1, 0, 0:1], 0.0, None, ALU.is_gt).then_inc(flag_ready, 1)
                dve.wait_ge(flag_ready, 1)
                general = dve.value_load(flag[0:1, 0:1], min_val=0, max_val=1)
                found = outb[0:EP, 0, 0:EC]
                with dve.If(general > 0):
                    with dve.Fori(0, E // KEY_LOAD) as n:
                        with dve.Fori(0, KEY_LOAD // PAIR_KEYS) as m:
                            c = n * (KEY_LOAD // PAIR_KEYS) + m
                            eq = adj[0:EP, 1, :].rearrange("p (e k) -> p e k", k=PAIR_KEYS)
                            mine = key[0:EP, own].unsqueeze(2).broadcast_to([EP, EC, PAIR_KEYS])
                            all_of = bias[0:EP, bass.ds(m * PAIR_KEYS, PAIR_KEYS)].unsqueeze(1).broadcast_to([EP, EC, PAIR_KEYS])
                            dve.wait_ge(keys_in, (n + 1) * 16)
                            nc.vector.tensor_tensor(eq, mine, all_of, ALU.is_equal).then_inc(keys_used, 1)
                            dve.wait_ge(keys_used, c + 2)
                            nc.vector.tensor_reduce(found, eq.bitcast(F32), AX_X, ALU.add).then_inc(pair_eq, 1)
                            dve.wait_ge(pair_eq, c + 1)
                            nc.vector.tensor_tensor(pairs[0:EP, :], pairs[0:EP, :], found, ALU.add).then_inc(pair_sum, 1)
                            dve.wait_ge(pair_sum, c + 1)
                nc.vector.memset(bad[0:EP, 1:2], 0.0).then_inc(flag_ready, 1)

            def repeats(b):
                STEPS = 9
                cols = bass.ds(b * BATCH, BATCH)
                before, behind, times, skip = (repeat[0:EP, k, :] for k in range(4))
                eq = adj[0:EP, 1, 0:BATCH * WINDOW].rearrange("p (c w) -> p c w", w=WINDOW)
                own = key[0:EP, bass.ds(b * BATCH + WINDOW, BATCH)].unsqueeze(2).broadcast_to([EP, BATCH, WINDOW])
                for k, (first, found) in enumerate(((0, before), (WINDOW + 1, behind))):
                    near = windows(key[0:EP, bass.ds(b * BATCH + first, BATCH)])
                    nc.vector.tensor_tensor(eq, own, near, ALU.is_equal).then_inc(same, 1)
                    dve.wait_ge(same, b * STEPS + 2 * k + 1)
                    nc.vector.tensor_reduce(found, eq.bitcast(F32), AX_X, ALU.add).then_inc(same, 1)
                    dve.wait_ge(same, b * STEPS + 2 * k + 2)
                nc.vector.scalar_tensor_tensor(times, before, 1.0, behind, ALU.add, ALU.add).then_inc(same, 1)
                nc.vector.tensor_scalar(skip, before, 0.0, float(SKIP), ALU.is_gt, ALU.mult).then_inc(same, 1)
                dve.wait_ge(same, b * STEPS + 6)
                nc.vector.tensor_tensor(mult[0:EP, cols], times, pairs[0:EP, cols], ALU.max).then_inc(same, 1)
                nc.vector.tensor_tensor(idx_out[0:EP, cols], idx_out[0:EP, cols], skip, ALU.add).then_inc(same, 1)
                dve.wait_ge(same, b * STEPS + 8)
                nc.vector.tensor_tensor(loops[0:EP, cols], loops[0:EP, cols], mult[0:EP, cols], ALU.add).then_inc(same, 1)
                dve.wait_ge(same, b * STEPS + 9)
                nc.vector.tensor_tensor(idx_in[0:EP, cols], idx_in[0:EP, cols], skip, ALU.add).then_inc(batch_ready, 1)
                dve.wait_ge(batch_ready, b + 1)

            def windows(ap):
                return bass.AP(tensor=ap.tensor, offset=ap.offset, ap=[*ap.ap, [1, WINDOW]])

            def sum_in(t, pair, s):
                dve.wait_ge(adj_full[s], 16 * (pair + 1))
                nc.vector.tensor_reduce(in_part[:, s, :], adj[:, s, :].bitcast(F32).rearrange("p (a r) -> p r a", r=P), AX_X, ALU.add
                                        ).then_inc(in_part_done, 1)

            def inverse(t, s):
                nc.vector.tensor_scalar(degc[:, s:s + 1], count[:, s, 0:1], 1.0, None, ALU.max).then_inc(deg_step, 1)
                dve.wait_ge(deg_step, 2 * t + 1)
                nc.vector.reciprocal(dinv[:, bass.ds(t, 1)], degc[:, s:s + 1]).then_inc(deg_step, 1)
                dve.wait_ge(deg_step, 2 * t + 2)

            def sum_out(t, s):
                nc.vector.tensor_reduce(dpart[:, s, :], adj[:, s, :].bitcast(F32).rearrange("p (a r) -> p a r", r=P), AX_X, ALU.add
                                        ).then_inc(dsum_part, 1)
                dve.wait_ge(dsum_part, t + 1)
                nc.vector.tensor_tensor(dsum[:, :], dsum[:, :], dpart[:, s, :], ALU.add).then_inc(dsum_done, 1)
                dve.wait_ge(dsum_done, t + 1)

            def block_stats(s, c):
                cols = slice(c * PSUM_COLS, (c + 1) * PSUM_COLS)
                nc.vector.bn_stats(stats[:, s, c, :], outb[:, s, cols]).then_inc(stats_done, 1)

            def norm(q, t, s):
                n = (0 if q == MEAN1 else NT) + t + 1
                dve.wait_ge(stats_done, n * NC)
                nc.vector.memset(scrap_dve[:, :], 0.0)
                nc.vector.bn_aggr(mv[:, s, :], stats[:, s, :, :]).then_inc(mv_done, 1)
                dve.wait_ge(mv_done, n)
                nc.vector.tensor_scalar(var[:, s:s + 1], mv[:, s, 1:2], EPS, None, ALU.add).then_inc(rstd_step, 1)
                dve.wait_ge(std_done, n)
                nc.vector.reciprocal(rstd[:, s:s + 1], std[:, s:s + 1]).then_inc(rstd_step, 1)
                newton(rstd[:, s:s + 1], var[:, s:s + 1], std[:, s:s + 1], rstd_step, n * 6 - 4)
                width = PSUM_COLS if is_end(q, t) else D
                for c in range(0, D, width):
                    nc.vector.tensor_scalar(outb[:, s, c:c + width], outb[:, s, c:c + width], mv[:, s, 0:1], rstd[:, s:s + 1],
                                            ALU.subtract, ALU.mult).then_inc(norm_done, 1)

            def last_tile(q, t, pair, s):
                dve.wait_ge(stored[s], 16 * (STORE[q] * PAIRS + pair + 1))
                dve.wait_ge(xin_full[s], 16 * (XIN[q] * PAIRS + pair + 1))
                for c in range(NC):
                    cols = slice(c * PSUM_COLS, (c + 1) * PSUM_COLS)
                    dve.wait_ge(block_full, c + 1)
                    nc.vector.scalar_tensor_tensor(outb[:, s, cols], acc[:, s, cols], dscale[:, t:t + 1], xin[:, s, cols],
                                                   ALU.mult, ALU.add).then_inc(block_done, 1)
                    dve.wait_ge(block_done, c + 1)
                    block_stats(s, c)
                norm(q, t, s)

            def newton(root, value, spare, step, done):
                dve.wait_ge(step, done)
                nc.vector.tensor_tensor(spare, root, root, ALU.mult).then_inc(step, 1)
                dve.wait_ge(step, done + 1)
                nc.vector.tensor_tensor(spare, spare, value, ALU.mult).then_inc(step, 1)
                dve.wait_ge(step, done + 2)
                nc.vector.tensor_scalar(spare, spare, -0.5, 1.5, ALU.mult, ALU.add).then_inc(step, 1)
                dve.wait_ge(step, done + 3)
                nc.vector.tensor_tensor(root, root, spare, ALU.mult).then_inc(step, 1)
                dve.wait_ge(step, done + 4)

            def evict(q, t, pair, s):
                z = outb[:, s, :]
                if is_end(q, t):
                    last_tile(q, t, pair, s)
                    return
                if q in (NEIGH0, NEIGH1):
                    dve.wait_ge(u_hi_done, (0 if q == NEIGH0 else NT) + t + 1)
                    nc.vector.tensor_tensor(row(u_lo, t), acc[:, s, :], row(u_hi, t).bitcast(F32), ALU.subtract).then_inc(acc_free, 1)
                    return
                dve.wait_ge(acc_full, q * NT + t + 1)
                if q in STORE:
                    dve.wait_ge(stored[s], 16 * (STORE[q] * PAIRS + pair + 1))
                elif q == GCN_LIN:
                    dve.wait_ge(stored[s], 16 * ((STORE[MEAN1] + 1) * PAIRS + 1))
                if q in biases:
                    dve.wait_ge(bias_full, 16 * (list(biases).index(q) + 1))
                    nc.vector.tensor_tensor(z, acc[:, s, :], bias[:, :], ALU.add).then_inc(acc_free, 1)
                if q == SELF1:
                    dve.wait_ge(acc_free, SLOTS + q * NT + t + 1)
                    dve.wait_ge(xin_full[s], 16 * (XIN[q] * PAIRS + pair + 1))
                    nc.vector.tensor_tensor(z, z, xin[:, s, :], ALU.add).then_inc(res_done, 1)
                elif q == GCN_LIN:
                    dve.wait_ge(u_hi_done, 2 * NT + t + 1)
                    nc.vector.scalar_tensor_tensor(row(u_lo, t), z, dscale[:, bass.ds(t, 1)], row(u_hi, t).bitcast(F32),
                                                   ALU.mult, ALU.subtract).then_inc(u_lo_done, 1)
                elif q in AGG:
                    if q == MEAN0:
                        inverse(t, s)
                    scale = dscale if q == GCN_AGG else dinv
                    dve.wait_ge(xin_full[s], 16 * (XIN[q] * PAIRS + pair + 1))
                    nc.vector.scalar_tensor_tensor(z, acc[:, s, :], scale[:, bass.ds(t, 1)], xin[:, s, :], ALU.mult, ALU.add
                                                   ).then_inc(acc_free, 1)
                    dve.wait_ge(acc_free, SLOTS + q * NT + t + 1)
                    if q == MEAN0:
                        nc.vector.tensor_scalar(z, z, 0.0, None, ALU.max).then_inc(relu_done, 1)
                        sum_out(t, s)
                    else:
                        for c in range(NC):
                            block_stats(s, c)
                        norm(q, t, s)

            nc.vector.memset(eps[:, :], EPS).then_inc(eps_ready, 1)
            nc.vector.memset(ones[:, :], 1.0).then_inc(ones_ready, 1)
            nc.vector.memset(ones_nt[:, :], 1.0).then_inc(ones_ready, 1)
            nc.vector.memset(dsum[:, :], 0.0).then_inc(dsum_zero, 1)
            nc.vector.memset(pairs[:, :], 0.0).then_inc(keys_used, 1)
            for s in range(SLOTS):
                nc.vector.memset(degc[:, s:s + 1], 0.0).then_inc(acc_free, 1)
                nc.vector.memset(std[:, s:s + 1], 0.0).then_inc(stored[s], 16)
                nc.vector.memset(rstd[:, s:s + 1], 0.0).then_inc(xt_stored[s], 16)
            nc.vector.memset(scrap_dve[:, :], 0.0).then_inc(wt_copied, 1)
            dve.wait_ge(dsum_zero, 1)
            dve.wait_ge(keys_used, 1)
            edge_keys()
            turn_lo(TURN[NEIGH0], 0, 0)
            for c in range(KD):
                split_lo(LIN[NEIGH0], c, c)
                if c == 0:
                    edge_parts()
            edge_form()
            dve.wait_ge(cell_step, CELL_STEPS)
            for q in range(8):
                def body(t, pair, s, chunk, q=q):
                    last = isinstance(t, int) and t == NT - 1
                    if q == MEAN0:
                        sum_in(t, pair, s)
                    if q in TURN and not last:
                        turn_lo(TURN[q], t + 1, 1 - s)
                    elif last and q + 1 in TURN:
                        turn_lo(TURN[q + 1], 0, 0)
                    elif last and q + 1 in LIN:
                        for c in range(KD):
                            if c == KD // 2:
                                evict(q, t, pair, s)
                            split_lo(LIN[q + 1], c, c)
                        if q == NEIGH0:
                            repeats(t)
                        return
                    if q == NEIGH0:
                        repeats(t)
                    evict(q, t, pair, s)
                    if q in AGG and q + 1 in LIN and chunk is not None:
                        split_lo(LIN[q + 1], chunk, s)
                tiles(dve, body)
                if q == MEAN0:
                    nc.vector.tensor_scalar(dsum[:, :], dsum[:, :], 1.0, None, ALU.add).then_inc(dscale_step, 1)
                    dve.wait_ge(dsqrt_done, 1)
                    nc.vector.reciprocal(dscale[:, :], dsqrt[:, :]).then_inc(dscale_step, 1)
                    newton(dscale[:, :], dsum[:, :], dsqrt[:, :], dscale_step, 2)

        @block.tensor
        def _(pe):
            def turn_tile(q, t, pair, s):
                pe.wait_ge(xin_full[s], 16 * (XIN[q] * PAIRS + pair + 1))
                for k in range(KD):
                    ins = nc.tensor.transpose(turned[:, k * P:(k + 1) * P], xin[:, s, k * P:(k + 1) * P], ident[:, :])
                ins.then_inc(xt_turned, 1)

            def turn_weights(c, pair, s):
                pe.wait_ge(raw_full[s], gcn_wait(pair, s))
                pe.wait_ge(wt_copied, c + 1)
                for k in range(KD):
                    ins = nc.tensor.transpose(turned[:, k * P:(k + 1) * P], raw[:, s, k * P:(k + 1) * P], ident[:, :])
                ins.then_inc(wt_turned, 1)

            def linear(q, t, pair, s, chunk):
                l = LIN[q]
                last = isinstance(t, int) and t == NT - 1
                if q in TURN:
                    pe.wait_ge(xt_lo_done, TURN[q] * NT + t + 1)
                else:
                    pe.wait_ge(xt_full[s], 32 * ((0 if q == SELF0 else PAIRS) + pair + 1))
                pe.wait_ge(acc_free, q * NT + t + 1)
                high = [[(k, xt_hi, w_hi), (k, xt_lo, w_hi)] for k in range(KD)]
                low = [[(k, xt_hi, w_lo)] for k in range(KD)]
                lag = LAG if s == 0 else 0
                steps = sum((high[k] + (low[k - lag] if k >= lag else []) for k in range(KD)), []) + sum(low[KD - lag:], [])
                for i, (k, left, right) in enumerate(steps):
                    if q in TURN and not last and i == 2 * len(steps) // 3:
                        turn_tile(q, t + 1, pair + s, 1 - s)
                    if s == 0 and left is xt_hi:
                        pe.wait_ge(w_hi_done if right is w_hi else w_lo_done, l * KD + k + 1)
                    for n in range(NC):
                        cols = slice(n * PSUM_COLS, (n + 1) * PSUM_COLS)
                        ins = nc.tensor.matmul(acc[:, s, cols], left[:, s, k * P:(k + 1) * P], right[:, k, cols],
                                               start=(i == 0), stop=(i == len(steps) - 1))
                    if i == len(steps) - 1:
                        ins.then_inc(acc_full, 1)
                    elif s == SLOTS - 1 and right is w_lo:
                        ins.then_inc(w_used, 1)
                if q == SELF0 and chunk is not None:
                    turn_weights(chunk, pair, s)

            def aggregate(q, t, pair, s, exact):
                def typed(ap):
                    return ap.bitcast(F32) if exact else ap
                pe.wait_ge(acc_free, q * NT + t + 1)
                pe.wait_ge(adj_full[s], 16 * (AGG[q] * PAIRS + pair + 1))
                if is_end(q, t):
                    for n in range(NC):
                        cols = slice(n * PSUM_COLS, (n + 1) * PSUM_COLS)
                        for k in range(NT):
                            a = typed(adj[0:rows(k), s, k * P:(k + 1) * P])
                            for part in (u_hi, u_lo):
                                ins = nc.tensor.matmul(acc[:, s, cols], a, typed(part[0:rows(k), k, cols]),
                                                       start=(k == 0 and part is u_hi), stop=(k == NT - 1 and part is u_lo))
                        ins.then_inc(block_full, 1)
                    return
                for k in range(NT):
                    if k == 2 * NT // 3 and isinstance(t, int) and t == NT - 1 and q + 1 in LIN:
                        pe.wait_ge(wt_copied, KD + 1)
                        turn_tile(q + 1, 0, 0, 0)
                    if q == GCN_AGG and s == 0:
                        pe.wait_ge(u_lo_done, k + 1)
                    n_k = rows(k)
                    a = typed(adj[0:n_k, s, k * P:(k + 1) * P])
                    if q == MEAN0 and k == NT - 1:
                        pe.wait_ge(in_part_done, t + 1)
                        nc.tensor.matmul(count[:, s, 0:1], in_part[:, s, :], ones[:, :], start=True, stop=True)
                    for part in (u_hi, u_lo):
                        for n in range(NC):
                            cols = slice(n * PSUM_COLS, (n + 1) * PSUM_COLS)
                            ins = nc.tensor.matmul(acc[:, s, cols], a, typed(part[0:n_k, k, cols]),
                                                   start=(k == 0 and part is u_hi), stop=(k == NT - 1 and part is u_lo))
                ins.then_inc(acc_full, 1)

            pe.wait_ge(ident_ready, 1)
            pe.wait_ge(ones_ready, 1)
            turn_tile(NEIGH0, 0, 0, 0)
            pe.wait_ge(bad_ready, 1)
            nc.tensor.matmul(count[0:1, 0, 0:1], bad[0:EP, 0:1], ones[0:EP, :], start=True, stop=True).then_inc(bad_summed, 1)
            for q in range(8):
                if q in LIN:
                    tiles(pe, lambda t, pair, s, chunk, q=q: linear(q, t, pair, s, chunk))
                    continue
                if q == MEAN0:
                    pe.wait_ge(flag_ready, 2)
                    general = pe.value_load(flag[0:1, 0:1], min_val=0, max_val=1)
                with pe.If(general > 0):
                    tiles(pe, lambda t, pair, s, chunk, q=q: aggregate(q, t, pair, s, True))
                with pe.Else():
                    tiles(pe, lambda t, pair, s, chunk, q=q: aggregate(q, t, pair, s, False))


_INS = ["x", "src", "dst", "L0_gnn_W_self0", "L0_gnn_W_neigh0", "L0_gnn_b0", "L0_gnn_W_self1", "L0_gnn_W_neigh1", "L0_gnn_b1",
        "L1_gnn_W", "L1_gnn_b"]


def kernel(**inputs):
    import numpy as _np
    import concourse.bacc as _bacc
    from concourse import mybir as _mybir
    from concourse.bass_utils import run_bass_kernel_spmd as _run

    nc = _bacc.Bacc("TRN2", target_bir_lowering=False, num_devices=1)
    arrays, args = {}, []
    for name in _INS:
        a = _np.ascontiguousarray(inputs[name])
        arrays[f"in_{name}"] = a
        args.append(nc.dram_tensor(f"in_{name}", a.shape, _mybir.dt.from_np(a.dtype), kind="ExternalInput").ap())
    shape = inputs["x"].shape
    args.append(nc.dram_tensor("out", shape, _mybir.dt.float32, kind="ExternalOutput").ap())
    build(nc, *args)
    r = _run(nc, [arrays], core_ids=[0])
    return r.results[0]["out"]
```
